# Optimizing a Trainium2 kernel written in Bass

```python
import numpy as np
import jax
import jax.numpy as jnp

def _softmax(x, axis=-1):
    return jax.nn.softmax(x, axis=axis)

def _gelu(x):
    return jax.nn.gelu(x, approximate=True)

def _silu(x):
    return jax.nn.silu(x)

def _sigmoid(x):
    return jax.nn.sigmoid(x)

def _layernorm(x, axis=-1, eps=1e-05):
    m = jnp.mean(x, axis=axis, keepdims=True)
    v = jnp.var(x, axis=axis, keepdims=True)
    return (x - m) / jnp.sqrt(v + eps)

def _scatter_add(tgt, idx, src, axis=0):
    return tgt.at[idx].add(src)

def _segment_sum(src, seg, n):
    return jax.ops.segment_sum(src, seg, n)
kernel_name = 'mk_flamingo_gated_d1_seqx_r8_4c4abb'

def setup_inputs(seed: int=0):
    np.random.seed(seed)
    _w = jnp.asarray

    def _rec_inputs():
        import jax
        import jax.numpy as jnp
        _rk = jax.random.key(seed)
        x = 7.22e-05 + 1 * jax.random.normal(jax.random.fold_in(_rk, 1), (16, 128, 256), jnp.float32)
        _lenS = 128 - jax.random.randint(jax.random.fold_in(_rk, 7), (16,), 0, max(1, 128 // 4) + 1, jnp.int32)
        _lenS2 = 128 - jax.random.randint(jax.random.fold_in(_rk, 8), (16,), 0, max(1, 128 // 4) + 1, jnp.int32)
        _ctx_2048P = jax.random.normal(jax.random.fold_in(_rk, 11), (16, 16, 256), jnp.float32)
        _ctx_2048c = jax.random.dirichlet(jax.random.fold_in(_rk, 511), 0.3 * jnp.ones((16,), jnp.float32), (16, 128))
        _ctx_2048t = jnp.einsum('bsk,bkd->bsd', _ctx_2048c, _ctx_2048P)
        _ctx_2048t = _ctx_2048t * jax.lax.rsqrt(jnp.mean(jnp.square(_ctx_2048t)) + 1e-12) * 0.953939
        ctx_2048 = 4.13588e-05 + 0.999923 * (_ctx_2048t + 0.3 * jax.random.normal(jax.random.fold_in(_rk, 611), (16, 128, 256), jnp.float32))
        _g = jax.random.normal(jax.random.fold_in(_rk, 9001), (2, 1), jnp.float32)
        _g = jnp.sign(_g) * jnp.maximum(jnp.abs(_g), 1.0) + (_g == 0) * 1.0
        g_xattn = _g[0]
        g_ffn = _g[1]
        return (x, ctx_2048, g_xattn, g_ffn)
    x, ctx_2048, g_xattn, g_ffn = _rec_inputs()

    def _L0_xattn_setup():
        import jax, jax.numpy as jnp
        import numpy as np
        N_HEAD = 8
        key = jax.random.key(seed)
        k1, k2, k3 = jax.random.split(key, 3)
        B, D, L = (4, 128, 256)
        q = jax.random.normal(k1, (B, D, L), dtype=jnp.float32)
        k = jax.random.normal(k2, (B, D, L), dtype=jnp.float32)
        v = jax.random.normal(k3, (B, D, L), dtype=jnp.float32)
        gamma = jnp.ones((), dtype=jnp.float32)
        return {'q': q, 'k': k, 'v': v, 'gamma': gamma}
    _L0_xattn_all = _L0_xattn_setup()
    _L0_xattn_in = {k: v for k, v in _L0_xattn_all.items() if k in ('gamma',)}
    del _L0_xattn_all

    def _L0_ffn_setup():
        import jax, jax.numpy as jnp
        import numpy as np
        H = 256
        HQ = 16
        HKV = 4
        D = 128
        E = 32
        K = 4
        I = 128
        ISH = 128
        EPS = 1e-06
        THETA = 10000.0
        NORM_MIN = 1e-12

        def rmsnorm(x, w):
            xf = x.astype(jnp.float32)
            var = jnp.mean(xf * xf, axis=-1, keepdims=True)
            return w * (xf * jax.lax.rsqrt(var + EPS))

        def rotate_half(x):
            x1 = x[..., 0::2]
            x2 = x[..., 1::2]
            return jnp.stack((-x2, x1), axis=-1).reshape(x.shape)
        key = jax.random.key(seed)
        ks = jax.random.split(key, 14)
        s = 0.02
        B, S = (1, 128)
        return {'hidden_states': jax.random.normal(ks[0], (B, S, H), jnp.float32), 'ln1_w': jnp.ones((H,), jnp.float32), 'ln2_w': jnp.ones((H,), jnp.float32), 'wq': jax.random.normal(ks[1], (H, HQ * D), jnp.float32) * s, 'wk': jax.random.normal(ks[2], (H, HKV * D), jnp.float32) * s, 'wv': jax.random.normal(ks[3], (H, HKV * D), jnp.float32) * s, 'wo': jax.random.normal(ks[4], (HQ * D, H), jnp.float32) * s, 'gate_w': jax.random.normal(ks[5], (E, H), jnp.float32) * s, 'bias_e': jnp.zeros((E,), jnp.float32), 'weg': jax.random.normal(ks[6], (E, H, I), jnp.float32) * s, 'weu': jax.random.normal(ks[7], (E, H, I), jnp.float32) * s, 'wed': jax.random.normal(ks[8], (E, I, H), jnp.float32) * s, 'wsg': jax.random.normal(ks[9], (H, ISH), jnp.float32) * s, 'wsu': jax.random.normal(ks[10], (H, ISH), jnp.float32) * s, 'wsd': jax.random.normal(ks[11], (ISH, H), jnp.float32) * s}
    _L0_ffn_all = _L0_ffn_setup()
    _L0_ffn_in = {k: v for k, v in _L0_ffn_all.items() if k in ('ln1_w', 'ln2_w', 'wq', 'wk', 'wv', 'wo', 'gate_w', 'bias_e', 'weg', 'weu', 'wed', 'wsg', 'wsu', 'wsd')}
    del _L0_ffn_all
    return {'x': x, 'ctx_2048': ctx_2048, 'g_xattn': g_xattn, 'g_ffn': g_ffn, 'L0_xattn_gamma': _L0_xattn_in['gamma'], 'L0_ffn_ln1_w': _L0_ffn_in['ln1_w'], 'L0_ffn_ln2_w': _L0_ffn_in['ln2_w'], 'L0_ffn_wq': _L0_ffn_in['wq'], 'L0_ffn_wk': _L0_ffn_in['wk'], 'L0_ffn_wv': _L0_ffn_in['wv'], 'L0_ffn_wo': _L0_ffn_in['wo'], 'L0_ffn_gate_w': _L0_ffn_in['gate_w'], 'L0_ffn_bias_e': _L0_ffn_in['bias_e'], 'L0_ffn_weg': _L0_ffn_in['weg'], 'L0_ffn_weu': _L0_ffn_in['weu'], 'L0_ffn_wed': _L0_ffn_in['wed'], 'L0_ffn_wsg': _L0_ffn_in['wsg'], 'L0_ffn_wsu': _L0_ffn_in['wsu'], 'L0_ffn_wsd': _L0_ffn_in['wsd']}

def reference(x, ctx_2048, g_xattn, g_ffn, L0_xattn_gamma, L0_ffn_ln1_w, L0_ffn_ln2_w, L0_ffn_wq, L0_ffn_wk, L0_ffn_wv, L0_ffn_wo, L0_ffn_gate_w, L0_ffn_bias_e, L0_ffn_weg, L0_ffn_weu, L0_ffn_wed, L0_ffn_wsg, L0_ffn_wsu, L0_ffn_wsd):
    import jax
    import jax.numpy as jnp

    def _L0_xattn_ref(q, k, v, gamma):
        import jax, jax.numpy as jnp
        import numpy as np
        N_HEAD = 8
        B, Dq, Lq = q.shape
        Dv, Lk = (v.shape[-2], v.shape[-1])
        h = N_HEAD
        dq = Dq // h
        dv = Dv // h
        qh = q.reshape(B, h, dq, Lq)
        kh = k.reshape(B, h, dq, Lk)
        vh = v.reshape(B, h, dv, Lk)
        scale = 1.0 / jnp.sqrt(jnp.asarray(dq, dtype=q.dtype))
        qk = jnp.einsum('bhdq,bhdl->bhql', qh, kh) * scale
        sm = jax.nn.softmax(qk, axis=-1)
        ret = jnp.einsum('bhql,bhdl->bhdq', sm, vh)
        ret = ret.reshape(B, Dv, Lq)
        return gamma * ret

    def _L0_ffn_ref(hidden_states, ln1_w, ln2_w, wq, wk, wv, wo, gate_w, bias_e, weg, weu, wed, wsg, wsu, wsd):
        import jax, jax.numpy as jnp
        import numpy as np
        H = 256
        HQ = 16
        HKV = 4
        D = 128
        E = 32
        K = 4
        I = 128
        ISH = 128
        EPS = 1e-06
        THETA = 10000.0
        NORM_MIN = 1e-12

        def rmsnorm(x, w):
            xf = x.astype(jnp.float32)
            var = jnp.mean(xf * xf, axis=-1, keepdims=True)
            return w * (xf * jax.lax.rsqrt(var + EPS))

        def rotate_half(x):
            x1 = x[..., 0::2]
            x2 = x[..., 1::2]
            return jnp.stack((-x2, x1), axis=-1).reshape(x.shape)
        B, S, _ = hidden_states.shape
        resid = hidden_states
        x = rmsnorm(hidden_states, ln1_w)
        q = (x @ wq).reshape(B, S, HQ, D).transpose(0, 2, 1, 3)
        k = (x @ wk).reshape(B, S, HKV, D).transpose(0, 2, 1, 3)
        v = (x @ wv).reshape(B, S, HKV, D).transpose(0, 2, 1, 3)
        pos = jnp.arange(S, dtype=jnp.float32)
        inv_freq = 1.0 / THETA ** (jnp.arange(0, D, 2, dtype=jnp.float32) / D)
        ang = pos[:, None] * inv_freq[None, :]
        cos = jnp.repeat(jnp.cos(ang), 2, axis=-1)[None, None]
        sin = jnp.repeat(jnp.sin(ang), 2, axis=-1)[None, None]
        q = q * cos + rotate_half(q) * sin
        k = k * cos + rotate_half(k) * sin
        k = jnp.repeat(k, HQ // HKV, axis=1)
        v = jnp.repeat(v, HQ // HKV, axis=1)
        scores = jnp.einsum('bhqd,bhkd->bhqk', q, k) / jnp.sqrt(jnp.float32(D))
        causal = jnp.tril(jnp.ones((S, S), dtype=bool))
        scores = jnp.where(causal, scores, jnp.float32(-1000000000.0))
        attn = jax.nn.softmax(scores, axis=-1)
        o = jnp.einsum('bhqk,bhkd->bhqd', attn, v).transpose(0, 2, 1, 3).reshape(B, S, HQ * D)
        x = resid + o @ wo
        resid2 = x
        xn = rmsnorm(x, ln2_w)
        T = B * S
        xf = xn.reshape(T, H).astype(jnp.float32)
        router_logits = xf @ gate_w.T
        probs = jax.nn.softmax(router_logits, axis=-1)
        _, sel = jax.lax.top_k(probs + bias_e, K)
        rw = jnp.take_along_axis(probs, sel, axis=-1)
        rw = rw / jnp.maximum(jnp.sum(rw, axis=-1, keepdims=True), NORM_MIN)
        cw = jnp.zeros((T, E), jnp.float32).at[jnp.arange(T)[:, None], sel].set(rw)
        g = jnp.einsum('th,ehi->tei', xf, weg)
        u = jnp.einsum('th,ehi->tei', xf, weu)
        hmid = jax.nn.silu(g) * u * cw[:, :, None]
        moe_y = jnp.einsum('tei,eih->th', hmid, wed).reshape(B, S, H)
        shared = jax.nn.silu(xn @ wsg) * (xn @ wsu) @ wsd
        return resid2 + moe_y + shared
    x = x + jnp.tanh(g_xattn[0]) * _L0_xattn_ref(_layernorm(x, axis=-1), ctx_2048, ctx_2048, L0_xattn_gamma)
    x = x + jnp.tanh(g_ffn[0]) * _L0_ffn_ref(_layernorm(x, axis=-1), L0_ffn_ln1_w, L0_ffn_ln2_w, L0_ffn_wq, L0_ffn_wk, L0_ffn_wv, L0_ffn_wo, L0_ffn_gate_w, L0_ffn_bias_e, L0_ffn_weg, L0_ffn_weu, L0_ffn_wed, L0_ffn_wsg, L0_ffn_wsu, L0_ffn_wsd)
    return x

_drawn_inputs = setup_inputs


def setup_inputs(seed=0):
    import zlib

    import numpy as np

    out = dict(_drawn_inputs(seed))
    spreads = {'L0_ffn_ln1_w': (1.0, 0.2), 'L0_ffn_ln2_w': (1.0, 0.6), 'L0_ffn_bias_e': (0.0, 0.307)}
    factors = {'L0_ffn_wq': 2.819, 'L0_ffn_wk': 2.81, 'L0_ffn_gate_w': 4.151}
    for name, (base, spread) in spreads.items():
        noise = np.random.default_rng([zlib.crc32(name.encode()), seed]).standard_normal(out[name].shape)
        drawn = base * np.exp(spread * noise) if base else spread * noise
        out[name] = jnp.asarray(drawn.astype(out[name].dtype))
    for name, factor in factors.items():
        out[name] = (out[name] * factor).astype(out[name].dtype)
    return out
```

```python
from contextlib import ExitStack

import numpy as np

import concourse.bass as bass
from concourse import mybir

F32 = mybir.dt.float32
BF16 = mybir.dt.bfloat16
I32 = mybir.dt.int32
U32 = mybir.dt.uint32
ALU = mybir.AluOpType
ACT = mybir.ActivationFunctionType
AX = mybir.AxisListType

P = 128
NB, S, H = 16, 128, 256
KT = H // P
XH, XD, XL = 8, 16, 256
NPAR = 2
HQ, HKV, D = 16, 4, 128
GQ = HQ // HKV
E, TOPK, I = 32, 4, 128
EPS_LN, EPS_RMS, NORM_MIN = 1e-5, 1e-6, 1e-12
THETA = 10000.0
MASKED = -1e30

T = NB * S
REGION = T + P
SHARED_ROW = E * REGION
X_ROWS = SHARED_ROW + T
ROUTED_TILES = (T * TOPK - E) // P + E + 1
TILES = NB + ROUTED_TILES
Y_ROWS = TILES * P

COLS, _at = {}, 0
for _name, _n in (("ident", P), ("before", P), ("causal", P), ("q_cos", D), ("q_sin", D), ("k_cos", D),
                  ("k_sin", D), ("parity", 2), ("unit_row", 2), ("keep_row", 2), ("ones_mask", NPAR * 32),
                  ("iota_e", E), ("region", E), ("power", 2 * NB), ("tile_no", 1)):
    COLS[_name] = (_at, _at + _n)
    _at += _n
NCONST = _at



def constant_table():
    t = np.zeros((P, NCONST), np.float32)

    def put(name, value):
        a, b = COLS[name]
        t[:, a:b] = value

    p = np.arange(P)
    put("ident", np.eye(P))
    put("before", p[:, None] < p[None, :])
    put("causal", np.where(p[None, :] <= p[:, None], 0.0, MASKED))
    inv = (1.0 / THETA ** (np.arange(0, D, 2, dtype=np.float32) / np.float32(D))).astype(np.float32)
    ang = np.arange(S, dtype=np.float32)[:, None] * inv[None, :]
    cos = np.repeat(np.cos(ang), 2, axis=1)
    sin = np.repeat(np.sin(ang), 2, axis=1)
    sin[:, 0::2] *= -1
    scale = 1.0 / np.sqrt(np.float32(D))
    put("q_cos", cos * scale)
    put("q_sin", sin * scale)
    put("k_cos", cos)
    put("k_sin", sin)
    odd = (p // XD) % 2
    put("parity", np.stack([odd == 0, odd == 1], 1))
    first = np.stack([p % 32 == XD, p % 32 == 0], 1)
    put("unit_row", first)
    put("keep_row", ~first)
    half = np.arange(32) // XD
    put("ones_mask", np.concatenate([half == 0, half == 1])[None, :])
    put("iota_e", np.arange(E)[None, :])
    put("region", np.arange(E)[None, :] * REGION)
    put("power", -0.5)
    put("tile_no", p[:, None])
    return t


def row_of_head(parity):
    return XD if parity == 0 else 0


def build(nc, x, ctx_in, g_xattn, g_ffn, gamma, ln1_w, ln2_w, wq, wk, wv, wo, gate_wt, bias_e,
          weg, weu, wed, wsg, wsu, wsd, consts, out):
    x_rows = nc.dram_tensor("x_rows", (X_ROWS, H), F32, kind="Internal").ap()
    y_rows = nc.dram_tensor("y_rows", (Y_ROWS, H), F32, kind="Internal").ap()

    with ExitStack() as stack:
        def sb(name, shape, dt=F32):
            return stack.enter_context(nc.sbuf_tensor(name, shape, dt))

        def bank(name, n=1):
            return stack.enter_context(nc.psum_tensor(name, [P, n, 512], F32))

        def sem(name):
            return stack.enter_context(nc.semaphore(name))

        tab = sb("tab", [P, NCONST])
        col = {k: tab[:, a:b] for k, (a, b) in COLS.items()}
        ident = col["ident"]
        before16 = sb("before16", [P, P], BF16)
        causal16 = sb("causal16", [P, P], BF16)
        ident16 = sb("ident16", [P, P], BF16)
        ones16 = sb("ones16", [P, P], BF16)
        gates = sb("gates", [P, 3])
        tanhs = sb("tanhs", [P, 2])
        tgx = sb("tgx", [P, 1])
        lnw = sb("lnw", [P, 2, KT])
        bias_sb = sb("bias_sb", [P, E])
        x1 = sb("x1", [P, NB, H])
        stats = sb("stats", [P, 6])
        mv1 = sb("mv1", [P, 2])
        mv = sb("mv", [P, NB, 2])
        arg = sb("arg", [P, 2, NB])
        inv = sb("inv", [P, 2, NB])
        wq_sb = sb("wq_sb", [P, KT, HQ * D])
        wk_sb = sb("wk_sb", [P, KT, HKV * D])
        wv_sb = sb("wv_sb", [P, KT, HKV * D])
        gate_sb = sb("gate_sb", [P, KT, E])

        banks = bank("banks", 8)

        s_in = sem("s_in")
        s_x = [sem(f"s_x{i}") for i in range(4)]
        s_w = sem("s_w")

        with ExitStack() as px:
            def xsb(name, shape, dt=F32):
                return px.enter_context(nc.sbuf_tensor(name, shape, dt))

            ctxb = xsb("ctxb", [P, 2, XL])
            q_par = xsb("q_par", [P, 2, NPAR, XL])
            q_aug = xsb("q_aug", [P, 2, NPAR, XL])
            k_aug = xsb("k_aug", [P, 2, NPAR, XL])
            q_inv = xsb("q_inv", [P, NB, NPAR])
            negmax = xsb("negmax", [P, NPAR, 2, P])
            v_t = xsb("v_t", [P, 2, NPAR, 2, P])
            ones_par = xsb("ones_par", [P, NPAR, 32])
            probs = xsb("probs", [P, 4, 2, 2, XL])
            den_r = xsb("den_r", [P, XL])
            ret = xsb("ret", [P, XL])
            ret2 = xsb("ret2", [P, XL])

            s_ctx = [sem(f"s_ctx{i}") for i in range(2)]
            xs = {n: sem("x_" + n) for n in (
                "setup", "tanh", "st", "mv", "arg", "inv", "qinv", "q", "kaug", "scores", "max", "mt", "qaug",
                "tscores", "exp", "pv", "vtp", "vt", "rec", "ret", "x1", "st2", "mv2", "agg2", "arg2", "inv2", "cast")}
            block = px.enter_context(nc.Block())

            sc_b, t_b, pv_b, mt_b = banks[:, 0:2], (banks[:, 2:4], banks[:, 4:6]), banks[:, 6], banks[:, 7]
            pv_t = banks[:, 7, 0:2 * P]

            @block.sync
            def _(sp):
                sp.dma_start(tab[:], consts).then_inc(s_in, 16)
                for i in range(4):
                    q = NB // 4
                    sp.dma_start(x1[:, q * i:q * i + q, :],
                                 x[q * i:q * i + q].rearrange("b s h -> s b h")).then_inc(s_x[i], 16)
                for b in range(2):
                    sp.dma_start(ctxb[:, b], ctx_in[b]).then_inc(s_ctx[b], 16)
                for i, g in enumerate((g_xattn, g_ffn, gamma)):
                    sp.dma_start(gates[:, i:i + 1], g.partition_broadcast(P)).then_inc(s_in, 16)
                sp.dma_start(lnw[:, 0], ln1_w).then_inc(s_in, 16)
                sp.dma_start(lnw[:, 1], ln2_w).then_inc(s_in, 16)
                sp.dma_start(bias_sb[:], bias_e.partition_broadcast(P)).then_inc(s_in, 16)
                sp.dma_start(gate_sb[:], gate_wt).then_inc(s_w, 16)
                for w_sb, w in ((wk_sb, wk), (wv_sb, wv), (wq_sb, wq)):
                    sp.dma_start(w_sb[:], w.rearrange("(t p) n -> p t n", p=P)).then_inc(s_w, 16)

            def augment_keys(dve, b, u):
                dve.wait_ge(s_ctx[u], 8 * (b - u) + 16)
                if not isinstance(b, int) or b >= 2:
                    dve.wait_ge(xs["tscores"], 4 * b - 4)
                for e in range(NPAR):
                    nc.vector.tensor_scalar(k_aug[:, u, e], ctxb[:, u], col["keep_row"][:, e:e + 1],
                                            col["unit_row"][:, e:e + 1], ALU.mult, ALU.add).then_inc(xs["kaug"], 1)

            def inverse_roots(pool, arg_sem, inv_sem, n):
                pool.wait_ge(arg_sem, n)
                nc.gpsimd.tensor_tensor(inv[:, 0:n, :], arg[:, 0:n, :],
                                        col["power"].rearrange("p (a b) -> p a b", a=2)[:, 0:n], ALU.pow
                                        ).then_inc(inv_sem, 1)

            @block.gpsimd
            def _(pool):
                nc.gpsimd.memset(negmax[:], 0.0).then_inc(xs["setup"], 1)
                nc.gpsimd.memset(v_t[:], 0.0).then_inc(xs["setup"], 1)
                nc.gpsimd.memset(ones16[:], 1.0).then_inc(xs["setup"], 1)
                pool.wait_ge(s_in, 7 * 16)
                inverse_roots(pool, xs["arg"], xs["inv"], 1)
                inverse_roots(pool, xs["arg2"], xs["inv2"], 2)

            def queries(dve, b, u):
                if not isinstance(b, int) or b >= 2:
                    dve.wait_ge(xs["scores"], 4 * b - 4)
                for e in range(NPAR):
                    nc.vector.tensor_scalar(q_par[:, u, e], x1[:, b, :], mv[:, b, 0:1], q_inv[:, b, e:e + 1],
                                            ALU.subtract, ALU.mult).then_inc(xs["q"], 1)

            def maxima(dve, b, unit):
                par, half = unit // 2, unit % 2
                dve.wait_ge(xs["scores"], 4 * b + unit + 1)
                if not isinstance(b, int) or b >= 1:
                    dve.wait_ge(xs["mt"], b)
                first = 64 * half + row_of_head(par)
                nc.vector.tensor_reduce(
                    negmax[:, par, :, first:first + 33:32].rearrange("p t j -> p j t"),
                    sc_b.rearrange("p j (t l) -> p j t l", t=2), AX.X, ALU.max, negate=True
                ).then_inc(xs["max"], 1)

            def add_maxima(dve, b, u):
                dve.wait_ge(xs["mt"], b + 1)
                dve.wait_ge(xs["q"], 2 * b + 2)
                if not isinstance(b, int) or b >= 2:
                    dve.wait_ge(xs["tscores"], 4 * b - 4)
                nc.vector.tensor_tensor(q_aug[:, u], mt_b.rearrange("p (e q) -> p e q", e=NPAR), q_par[:, u],
                                        ALU.add).then_inc(xs["qaug"], 1)

            def divide(dve, b):
                dve.wait_ge(xs["pv"], 4 * b + 4)
                nc.vector.reciprocal(den_r[:], pv_b[:, XL:2 * XL]).then_inc(xs["rec"], 1)
                dve.wait_ge(xs["rec"], b + 1)
                nc.vector.tensor_tensor(ret[:], pv_b[:, 0:XL], den_r[:], ALU.mult).then_inc(xs["ret"], 1)

            def residual(dve, b):
                dve.wait_ge(xs["ret"], b + 1)
                nc.vector.scalar_tensor_tensor(ret2[:], ret[:], tgx[:], x1[:, b, :], ALU.mult, ALU.add
                                               ).then_inc(xs["x1"], 1)
                dve.wait_ge(xs["x1"], b + 1)
                nc.vector.bn_stats(stats[:], ret2[:]).then_inc(xs["st2"], 1)
                dve.wait_ge(xs["st2"], b + 1)
                nc.vector.tensor_scalar(x1[:, b, :], ret2[:], 1.0, None, ALU.mult)
                nc.vector.bn_aggr(mv1[:], stats[:]).then_inc(xs["agg2"], 1)
                dve.wait_ge(xs["agg2"], b + 1)
                nc.vector.tensor_scalar(mv[:, b, :], mv1[:], 1.0, None, ALU.mult).then_inc(xs["mv2"], 1)

            @block.vector
            def _(dve):
                for b in range(NB):
                    dve.wait_ge(s_x[b // 4], 16)
                    if b:
                        dve.wait_ge(xs["mv"], b)
                    nc.vector.bn_stats(stats[:], x1[:, b, :]).then_inc(xs["st"], 1)
                    dve.wait_ge(xs["st"], b + 1)
                    nc.vector.bn_aggr(mv[:, b, :], stats[:]).then_inc(xs["mv"], 1)
                dve.wait_ge(xs["mv"], NB)
                nc.vector.tensor_scalar_add(arg[:, 0, :], mv[:, :, 1], EPS_LN).then_inc(xs["arg"], 1)
                dve.wait_ge(s_in, 7 * 16)
                nc.vector.tensor_copy(before16[:], col["before"]).then_inc(xs["cast"], 1)
                nc.vector.tensor_copy(causal16[:], col["causal"]).then_inc(xs["cast"], 1)
                nc.vector.tensor_copy(ident16[:], ident).then_inc(xs["cast"], 1)
                nc.vector.tensor_copy(ones_par[:], col["ones_mask"].rearrange("p (a b) -> p a b", a=2)
                                      ).then_inc(xs["cast"], 1)
                dve.wait_ge(xs["tanh"], 1)
                nc.vector.tensor_tensor(tgx[:], tanhs[:, 0:1], gates[:, 2:3], ALU.mult).then_inc(xs["cast"], 1)
                dve.wait_ge(xs["inv"], 1)
                for e in range(NPAR):
                    nc.vector.tensor_scalar(q_inv[:, :, e], inv[:, 0, :], col["parity"][:, e:e + 1], None,
                                            ALU.mult).then_inc(xs["qinv"], 1)
                dve.wait_ge(xs["qinv"], 2)
                dve.wait_ge(xs["cast"], 5)
                dve.wait_ge(xs["setup"], 3)
                augment_keys(dve, 0, 0)
                queries(dve, 0, 0)
                queries(dve, 1, 1)
                for unit in range(4):
                    maxima(dve, 0, unit)

                def body(b, u, first=False, last=False, ahead=True):
                    add_maxima(dve, b, u)
                    if not first:
                        divide(dve, b - 1)
                    if not last:
                        maxima(dve, b + 1, 0)
                    if not first:
                        residual(dve, b - 1)
                    if not last:
                        maxima(dve, b + 1, 1)
                        augment_keys(dve, b + 1, 1 - u)
                        maxima(dve, b + 1, 2)
                        maxima(dve, b + 1, 3)
                    if ahead:
                        queries(dve, b + 2, u)

                body(0, 0, first=True)
                with dve.Fori(0, (NB - 4) // 2) as i:
                    b = 2 * i + 1
                    body(b, 1)
                    body(b + 1, 0)
                body(NB - 3, 1)
                body(NB - 2, 0, ahead=False)
                body(NB - 1, 1, last=True, ahead=False)
                divide(dve, NB - 1)
                residual(dve, NB - 1)
                dve.wait_ge(xs["mv2"], NB)
                nc.vector.tensor_scalar_add(arg[:, 0, :], mv[:, :, 1], EPS_LN).then_inc(xs["arg2"], 1)
                nc.vector.tensor_scalar(arg[:, 1, :], mv[:, :, 1], 1.0 + EPS_RMS, EPS_RMS * EPS_LN,
                                        ALU.mult, ALU.add).then_inc(xs["arg2"], 1)

            def scores(pe, b, u, unit):
                par, half = unit // 2, unit % 2
                pe.wait_ge(xs["q"], 2 * b + par + 1)
                if unit == 0:
                    pe.wait_ge(s_ctx[u], 8 * (b - u) + 16)
                if unit or not isinstance(b, int) or b >= 1:
                    pe.wait_ge(xs["max"], 4 * b + unit)
                for j in range(2):
                    r = 64 * half + 32 * j
                    for t in range(2):
                        last = nc.tensor.matmul(sc_b[:, j, t * XL:(t + 1) * XL], q_par[r:r + 32, u, par, t * P:(t + 1) * P],
                                                ctxb[r:r + 32, u], start=True, stop=True)
                last.then_inc(xs["scores"], 1)

            def transpose_values(pe, b, u):
                if not isinstance(b, int) or b >= 1:
                    pe.wait_ge(xs["qaug"], b)
                pe.wait_ge(s_ctx[u], 8 * (b - u) + 16)
                for t in range(2):
                    last = nc.tensor.transpose(pv_t[:, t * P:(t + 1) * P], ctxb[:, u, t * P:(t + 1) * P], ident)
                last.then_inc(xs["vtp"], 1)

            def transpose_maxima(pe, b):
                pe.wait_ge(xs["max"], 4 * b + 4)
                for par in range(NPAR):
                    for t in range(2):
                        last = nc.tensor.transpose(mt_b[:, par * XL + t * P:par * XL + (t + 1) * P],
                                                   negmax[:, par, t], ident)
                last.then_inc(xs["mt"], 1)

            def shifted_scores(pe, b, u, unit):
                par, half = unit // 2, unit % 2
                pe.wait_ge(xs["qaug"], b + 1)
                pe.wait_ge(xs["kaug"], 2 * b + par + 1)
                if unit >= 2 or not isinstance(b, int) or b >= 1:
                    pe.wait_ge(xs["exp"], 4 * b + unit - 1)
                for j in range(2):
                    r = 64 * half + 32 * j
                    for t in range(2):
                        last = nc.tensor.matmul(t_b[unit % 2][:, j, t * XL:(t + 1) * XL],
                                                k_aug[r:r + 32, u, par, t * P:(t + 1) * P],
                                                q_aug[r:r + 32, u, par], start=True, stop=True)
                last.then_inc(xs["tscores"], 1)

            def weigh_values(pe, b, u, unit):
                par, half = unit // 2, unit % 2
                pe.wait_ge(xs["exp"], 4 * b + unit + 1)
                if unit == 0:
                    if not isinstance(b, int) or b >= 1:
                        pe.wait_ge(xs["ret"], b)
                for t in range(2):
                    for j in range(2):
                        r = 64 * half + 32 * j
                        nc.tensor.matmul(pv_b[r:r + 32, 0:XL], v_t[:, u, par, t, r:r + 32], probs[:, unit, j, t],
                                         start=(par == 0 and t == 0), stop=(par == 1 and t == 1), skip_group_check=True)
                for t in range(2):
                    for j in range(2):
                        r = 64 * half + 32 * j
                        last = nc.tensor.matmul(pv_b[r:r + 32, XL:2 * XL], ones_par[:, par], probs[:, unit, j, t],
                                                start=False, stop=(par == 1 and t == 1), skip_group_check=True)
                last.then_inc(xs["pv"], 1)

            @block.tensor
            def _(pe):
                pe.wait_ge(s_in, 7 * 16)
                pe.wait_ge(xs["cast"], 5)
                transpose_values(pe, 0, 0)
                for unit in range(4):
                    scores(pe, 0, 0, unit)

                def body(b, u, last=False):
                    pe.wait_ge(xs["vt"], 2 * b + 2)
                    transpose_maxima(pe, b)
                    shifted_scores(pe, b, u, 0)
                    shifted_scores(pe, b, u, 1)
                    if not last:
                        scores(pe, b + 1, 1 - u, 0)
                    shifted_scores(pe, b, u, 2)
                    weigh_values(pe, b, u, 0)
                    if not last:
                        scores(pe, b + 1, 1 - u, 1)
                    shifted_scores(pe, b, u, 3)
                    weigh_values(pe, b, u, 1)
                    if not last:
                        scores(pe, b + 1, 1 - u, 2)
                        transpose_values(pe, b + 1, 1 - u)
                    weigh_values(pe, b, u, 2)
                    if not last:
                        scores(pe, b + 1, 1 - u, 3)
                    weigh_values(pe, b, u, 3)

                body(0, 0)
                with pe.Fori(0, (NB - 2) // 2) as i:
                    body(2 * i + 1, 1)
                    body(2 * i + 2, 0)
                body(NB - 1, 1, last=True)

            def exponentials(act, b, unit):
                act.wait_ge(xs["tscores"], 4 * b + unit + 1)
                if not isinstance(b, int) or b >= 1:
                    act.wait_ge(xs["pv"], 4 * b + unit - 3)
                nc.scalar.activation(probs[:, unit], t_b[unit % 2].rearrange("p j (t l) -> p j t l", t=2), ACT.Exp,
                                     scale=XD ** -0.5).then_inc(xs["exp"], 1)

            def keep_values(act, b, u):
                act.wait_ge(xs["vtp"], b + 1)
                if not isinstance(b, int) or b >= 2:
                    act.wait_ge(xs["pv"], 4 * b - 4)
                for par in range(NPAR):
                    src = pv_t[:, 0:2 * P].rearrange("p (t j n) -> p t j n", t=2, j=4)
                    dst = v_t[:, u, par].rearrange("p t (j n) -> p t j n", j=4)
                    nc.scalar.copy(dst[:, :, :, par * XD:par * XD + XD], src[:, :, :, par * XD:par * XD + XD]
                                   ).then_inc(xs["vt"], 1)

            @block.scalar
            def _(act):
                act.wait_ge(s_in, 7 * 16)
                nc.scalar.activation(tanhs[:], gates[:, 0:2], ACT.Tanh).then_inc(xs["tanh"], 1)
                act.wait_ge(xs["setup"], 3)
                keep_values(act, 0, 0)

                def load_context(b, u):
                    act.wait_ge(xs["scores"], 4 * b - 4)
                    act.wait_ge(xs["vtp"], b - 1)
                    act.wait_ge(xs["kaug"], 2 * b - 2)
                    act.dma_start(ctxb[:, u], ctx_in[b]).then_inc(s_ctx[u], 16)

                def body(b, u, ahead=True, last=False):
                    if ahead:
                        load_context(b + 2, u)
                    for unit in range(4):
                        exponentials(act, b, unit)
                    if not last:
                        keep_values(act, b + 1, 1 - u)

                body(0, 0)
                with act.Fori(0, (NB - 4) // 2) as i:
                    body(2 * i + 1, 1)
                    body(2 * i + 2, 0)
                body(NB - 3, 1)
                body(NB - 2, 0, ahead=False)
                body(NB - 1, 1, ahead=False, last=True)
        nc.all_engine_barrier()

        gu = sb("gu", [P, E + 1, KT, 2 * I])
        dn = sb("dn", [P, E + 1, H])
        oh_all = sb("oh_all", [P, NB, TOPK, E])
        slots_all = sb("slots_all", [P, NB, TOPK])
        rw_all = sb("rw_all", [P, NB, TOPK])
        counts = sb("counts", [P, E])
        counts16 = sb("counts16", [P, E], BF16)
        tick_v = sb("tick_v", [P, 2])
        tick_p = sb("tick_p", [P, 3])
        wsem = sem("moe_weights")
        wsem2 = sem("moe_weights2")
        s_sh = [sem(f"shared_rows{i}") for i in range(2)]
        s_sc = [sem(f"scattered{i}") for i in range(2)]

        def hold_v():
            nc.vector.tensor_copy(tick_v[:, 0:1], tick_v[:, 1:2])

        def hold_p(u=0):
            return nc.gpsimd.tensor_tensor(tick_p[:, u:u + 1], tick_p[:, 2:3], tick_p[:, 2:3], ALU.add)

        def load_expert_weights(sp, lo, hi, done):
            sp.dma_start(gu[:, lo:hi, :, 0:I], weg[lo:hi].rearrange("e (t p) i -> p (e t) i", p=P)).then_inc(done, 16)
            sp.dma_start(gu[:, lo:hi, :, I:2 * I], weu[lo:hi].rearrange("e (t p) i -> p (e t) i", p=P)).then_inc(done, 16)

        EARLY = E // 2

        with ExitStack() as pf:
            def fsb(name, shape, dt=F32):
                return pf.enter_context(nc.sbuf_tensor(name, shape, dt))

            late = gu[:, EARLY:E].rearrange("p e t n -> p (e t n)")
            q_t = late[:, 0:2 * HQ * S].rearrange("p (u h s) -> p u h s", u=2, h=HQ)
            o_t = late[:, 4096:4096 + HQ * S].rearrange("p (h s) -> p h s", h=HQ)
            k_t = late[:, 6144:6144 + 2 * HKV * S].rearrange("p (u h s) -> p u h s", u=2, h=HKV)
            v_sb = fsb("v_sb", [P, 2, HKV * D])
            wo_sb = fsb("wo_sb", [P, HQ, H])
            zr = fsb("zr", [P, H])
            h_t = fsb("h_t", [P, KT, S])
            r_cos = fsb("r_cos", [P, GQ * D])
            r_sin = fsb("r_sin", [P, GQ * D])
            roped = fsb("roped", [P, 2, GQ * D])
            pr = fsb("pr", [P, 2, GQ, S])
            pn = fsb("pn", [P, GQ, S])
            p_t = fsb("p_t", [P, GQ, S])
            negmax = fsb("fnegmax", [P, 2, GQ])
            sums = fsb("sums", [P, 2, GQ])
            rsums = fsb("rsums", [P, GQ])
            z = fsb("z", [P, H])
            r2 = fsb("r2", [P, H])
            xn = fsb("xn", [P, 2, H])
            xf_t = fsb("xf_t", [P, KT, S])
            rms_arg = fsb("rms_arg", [P, 2])
            rms_inv = fsb("rms_inv", [P, 1])
            rneg = fsb("rneg", [P, 1])
            rsum = fsb("rsum", [P, 1])
            rrec = fsb("rrec", [P, 1])
            rexp = fsb("rexp", [P, E])
            biased = fsb("biased", [P, E])
            top8 = fsb("top8", [P, 8])
            idx8 = fsb("idx8", [P, 8], U32)
            idxf = fsb("idxf", [P, TOPK])
            oh = fsb("oh", [P, TOPK, E])
            mask16 = fsb("mask16", [P, E], BF16)
            both = fsb("both", [P, 2, E])
            prod = fsb("prod", [P, 2, TOPK, E])
            picked = fsb("picked", [P, 2, TOPK])
            islot = fsb("islot", [P, 2, TOPK], I32)
            wsum = fsb("wsum", [P, 1])
            wmax = fsb("wmax", [P, 1])
            wrec = fsb("wrec", [P, 1])

            fs = {n: sem("f_" + n) for n in (
                "wo", "init", "pool_init", "zr", "htp", "ht", "proj", "cs", "rope", "v", "tp", "qk", "s", "max", "exp", "rinv",
                "norm", "ptp", "pt", "otp", "ot", "y", "resid", "rstd", "xn", "rtp", "rt", "logit", "rmax", "rexp",
                "route", "prefix", "slot", "mix", "weights")}
            block = pf.enter_context(nc.Block())
            pj_b, tp_b, pt_b, s_b, o_b, m_b = (banks[:, 0], banks[:, 1]), banks[:, 2], banks[:, 3], \
                (banks[:, 4], banks[:, 5]), banks[:, 6], banks[:, 7]

            def later(b, n=1):
                return not isinstance(b, int) or b >= n

            @block.sync
            def _(sp):
                sp.dma_start(wo_sb[:], wo.rearrange("(h d) n -> d h n", d=D)).then_inc(fs["wo"], 16)
                sp.dma_start(gu[:, E, :, 0:I], wsg.rearrange("(t p) i -> p t i", p=P)).then_inc(wsem, 16)
                sp.dma_start(gu[:, E, :, I:2 * I], wsu.rearrange("(t p) i -> p t i", p=P)).then_inc(wsem, 16)
                sp.dma_start(dn[:, E], wsd).then_inc(wsem, 16)
                load_expert_weights(sp, 0, EARLY, wsem)
                sp.dma_start(dn[:, 0:E], wed.rearrange("e i h -> i e h")).then_inc(wsem, 16)

            def pe_head_transpose(pe, b):
                pe.wait_ge(fs["zr"], b + 1)
                if later(b):
                    pe.wait_ge(fs["qk"], 5 * b)
                for t in range(KT):
                    last = nc.tensor.transpose(tp_b[:, t * P:(t + 1) * P], zr[:, t * P:(t + 1) * P], ident)
                last.then_inc(fs["htp"], 1)

            def pe_project(pe, b, c):
                if c == 0:
                    pe.wait_ge(fs["ht"], 2 * b + 2)
                if c == 0 and later(b):
                    pe.wait_ge(fs["cs"], 10 * b - 2)
                if c == 1 and later(b):
                    pe.wait_ge(fs["cs"], 10 * b)
                if c == 2:
                    pe.wait_ge(fs["cs"], 10 * b + 2)
                if c == 3:
                    pe.wait_ge(fs["v"], b + 1)
                if c >= 4:
                    pe.wait_ge(fs["cs"], 10 * b + 2 * (c - 2))
                w = (wk_sb, wv_sb)[c] if c < 2 else wq_sb
                at = max(c - 2, 0) * GQ * D
                for t in range(KT):
                    last = nc.tensor.matmul(pj_b[c % 2], h_t[:, t], w[:, t, at:at + GQ * D], start=(t == 0), stop=(t == KT - 1))
                last.then_inc(fs["proj"], 1)

            def pe_chunk_transpose(pe, b, r):
                pe.wait_ge(fs["rope"], 5 * b + r + 1)
                if r == 0:
                    pe.wait_ge(fs["ht"], 2 * b + 2)
                else:
                    pe.wait_ge(fs["qk"], 5 * b + r)
                for j in range(GQ):
                    last = nc.tensor.transpose(tp_b[:, j * P:(j + 1) * P], roped[:, r % 2, j * D:(j + 1) * D], ident)
                last.then_inc(fs["tp"], 1)

            def pe_scores(pe, b, u, g):
                if g == 0:
                    pe.wait_ge(fs["qk"], 5 * b + 5)
                if g >= 2:
                    pe.wait_ge(fs["exp"], 16 * b + 4 * (g - 1))
                elif later(b):
                    pe.wait_ge(fs["exp"], 16 * b - 8 + 4 * (g + 1))
                nc.tensor.matmul(s_b[g % 2].rearrange("p (h s) -> p h s", h=GQ), ident16[:],
                                 causal16[:].unsqueeze(1).to_broadcast([P, GQ, S]), start=True, stop=False)
                for j in range(GQ):
                    last = nc.tensor.matmul(s_b[g % 2][:, j * S:(j + 1) * S], q_t[:, u, g * GQ + j], k_t[:, u, g],
                                            start=False, stop=(j == GQ - 1))
                last.then_inc(fs["s"], 1)

            def pe_probs_transpose(pe, b, g):
                pe.wait_ge(fs["norm"], 4 * b + g + 1)
                if g or later(b):
                    pe.wait_ge(fs["pt"], 4 * b + g)
                for j in range(GQ):
                    last = nc.tensor.transpose(pt_b[:, j * S:(j + 1) * S], pn[:, j], ident)
                last.then_inc(fs["ptp"], 1)

            def pe_weigh(pe, b, u, g):
                pe.wait_ge(fs["pt"], 4 * b + g + 1)
                if g or later(b):
                    pe.wait_ge(fs["ot"], 4 * b + g)
                nc.tensor.matmul(o_b, v_sb[:, u, g * D:(g + 1) * D], p_t[:].rearrange("p h s -> p (h s)"),
                                 start=True, stop=True).then_inc(fs["otp"], 1)

            def pe_out(pe, b, lo, hi):
                if lo == 0:
                    if later(b):
                        pe.wait_ge(fs["slot"], 3 * b - 2)
                    else:
                        pe.wait_ge(fs["wo"], 16)
                pe.wait_ge(fs["ot"], 4 * b + hi // GQ)
                for h in range(lo, hi):
                    last = nc.tensor.matmul(m_b[:, 0:H], o_t[:, h], wo_sb[:, h], start=(h == 0), stop=(h == HQ - 1))
                if hi == HQ:
                    last.then_inc(fs["y"], 1)

            def pe_router_transpose(pe, b, u):
                pe.wait_ge(fs["xn"], b + 1)
                for t in range(KT):
                    last = nc.tensor.transpose(m_b[:, H + t * P:H + (t + 1) * P], xn[:, u, t * P:(t + 1) * P], ident)
                last.then_inc(fs["rtp"], 1)

            def pe_logits(pe, b):
                pe.wait_ge(fs["rt"], 2 * b + 2)
                for t in range(KT):
                    last = nc.tensor.matmul(m_b[:, 0:E], xf_t[:, t], gate_sb[:, t], start=(t == 0), stop=(t == KT - 1))
                last.then_inc(fs["logit"], 1)

            def pe_prefix(pe, b):
                pe.wait_ge(fs["route"], 8 * b + 8)
                pe.wait_ge(fs["rexp"], b + 1)
                nc.tensor.matmul(m_b[:, 0:E], before16[:], mask16[:], start=True, stop=False)
                nc.tensor.matmul(m_b[:, 0:E], ones16[:], counts16[:], start=False, stop=True).then_inc(fs["prefix"], 1)

            def act_copy_scaled(dst, src, w, done):
                for t in range(KT):
                    nc.scalar.activation(dst[:, t], src[:, t * P:(t + 1) * P], ACT.Copy, scale=lnw[:, w, t:t + 1]
                                         ).then_inc(done, 1)

            def act_head_transpose(act, b):
                act.wait_ge(fs["htp"], b + 1)
                if later(b):
                    act.wait_ge(fs["proj"], 6 * b)
                act_copy_scaled(h_t, tp_b, 0, fs["ht"])

            def act_router_transpose(act, b):
                act.wait_ge(fs["rtp"], b + 1)
                if later(b):
                    act.wait_ge(fs["logit"], b)
                act_copy_scaled(xf_t, m_b[:, H:2 * H], 1, fs["rt"])

            def act_values(act, b, u):
                act.wait_ge(fs["proj"], 6 * b + 2)
                if later(b, 2):
                    act.wait_ge(fs["otp"], 4 * b - 4)
                nc.scalar.copy(v_sb[:, u], pj_b[1]).then_inc(fs["v"], 1)

            def act_chunk(act, b, u, r):
                act.wait_ge(fs["tp"], 5 * b + r + 1)
                if later(b, 2):
                    act.wait_ge(fs["s"], 4 * b - 4)
                dst = k_t[:, u] if r == 0 else q_t[:, u, (r - 1) * GQ:r * GQ]
                nc.scalar.copy(dst.rearrange("p h s -> p (h s)"), tp_b).then_inc(fs["qk"], 1)

            def act_exp(act, b, g):
                act.wait_ge(fs["max"], 4 * b + g + 1)
                if g >= 2:
                    act.wait_ge(fs["norm"], 4 * b + g - 1)
                elif later(b):
                    act.wait_ge(fs["norm"], 4 * b + g - 1)
                for j in range(GQ):
                    nc.scalar.activation(pr[:, g % 2, j], s_b[g % 2][:, j * S:(j + 1) * S], ACT.Exp,
                                         bias=negmax[:, g % 2, j:j + 1], accum_out=sums[:, g % 2, j:j + 1]
                                         ).then_inc(fs["exp"], 1)

            def act_probs(act, b, g):
                act.wait_ge(fs["ptp"], 4 * b + g + 1)
                if g or later(b):
                    act.wait_ge(fs["otp"], 4 * b + g)
                nc.scalar.copy(p_t[:].rearrange("p h s -> p (h s)"), pt_b).then_inc(fs["pt"], 1)

            def act_weighed(act, b, g):
                act.wait_ge(fs["otp"], 4 * b + g + 1)
                if later(b):
                    act.wait_ge(fs["y"], b)
                nc.scalar.copy(o_t[:, g * GQ:(g + 1) * GQ].rearrange("p h s -> p (h s)"), o_b).then_inc(fs["ot"], 1)

            def act_route(act, b):
                act.wait_ge(fs["rmax"], b + 1)
                nc.scalar.activation(rexp[:], m_b[:, 0:E], ACT.Exp, bias=rneg[:], accum_out=rsum[:]
                                     ).then_inc(fs["rexp"], 1)

            def dve_norm_rows(dve, b):
                if later(b):
                    dve.wait_ge(fs["htp"], b)
                nc.vector.tensor_scalar(zr[:], x1[:, b, :], mv[:, b, 0:1], inv[:, 1, bass.ds(b, 1)], ALU.subtract, ALU.mult
                                        ).then_inc(fs["zr"], 1)

            def dve_rotate(dve, b, r):
                c = 0 if r == 0 else r + 1
                bank = pj_b[c % 2]
                dve.wait_ge(fs["proj"], 6 * b + c + 1)
                if r or later(b):
                    dve.wait_ge(fs["rope"], 5 * b + r)
                cs, sn = ("k_cos", "k_sin") if r == 0 else ("q_cos", "q_sin")
                nc.vector.tensor_tensor(r_cos[:].rearrange("p (h d) -> p h d", h=GQ), bank.rearrange("p (h d) -> p h d", h=GQ),
                                        col[cs].unsqueeze(1).to_broadcast([P, GQ, D]), ALU.mult).then_inc(fs["cs"], 1)
                pairs = "p (h d two) -> p h d two"
                nc.vector.tensor_tensor(
                    r_sin[:].rearrange(pairs, h=GQ, two=2), bank.rearrange(pairs, h=GQ, two=2)[:, :, :, ::-1],
                    col[sn].rearrange("p (d two) -> p d two", two=2).unsqueeze(1).to_broadcast([P, GQ, D // 2, 2]),
                    ALU.mult).then_inc(fs["cs"], 1)

            def dve_max(dve, b, g):
                dve.wait_ge(fs["s"], 4 * b + g + 1)
                nc.vector.tensor_reduce(negmax[:, g % 2], s_b[g % 2].rearrange("p (h s) -> p h s", h=GQ), AX.X, ALU.max,
                                        negate=True).then_inc(fs["max"], 1)

            def dve_normalize(dve, b, g):
                dve.wait_ge(fs["exp"], 16 * b + 4 * g + 4)
                if g or later(b):
                    dve.wait_ge(fs["norm"], 4 * b + g)
                nc.vector.reciprocal(rsums[:], sums[:, g % 2]).then_inc(fs["rinv"], 1)
                dve.wait_ge(fs["rinv"], 4 * b + g + 1)
                if g or later(b):
                    dve.wait_ge(fs["ptp"], 4 * b + g)
                nc.vector.tensor_tensor(pn[:], pr[:, g % 2], rsums[:].unsqueeze(2).to_broadcast([P, GQ, S]), ALU.mult
                                        ).then_inc(fs["norm"], 1)

            def dve_residual(dve, b):
                R = 7 * b
                nc.vector.tensor_scalar(z[:], x1[:, b, :], mv[:, b, 0:1], inv[:, 0, bass.ds(b, 1)], ALU.subtract, ALU.mult
                                        ).then_inc(fs["resid"], 1)
                dve.wait_ge(fs["y"], b + 1)
                dve.wait_ge(fs["resid"], R + 1)
                nc.vector.tensor_tensor(r2[:], m_b[:, 0:H], z[:], ALU.add).then_inc(fs["resid"], 1)
                dve.wait_ge(fs["resid"], R + 2)
                nc.vector.bn_stats(stats[:], r2[:]).then_inc(fs["resid"], 1)
                dve.wait_ge(fs["resid"], R + 3)
                nc.vector.scalar_tensor_tensor(x1[:, b, :], r2[:], tanhs[:, 1:2], x1[:, b, :], ALU.mult, ALU.add
                                               ).then_inc(fs["resid"], 1)
                nc.vector.bn_aggr(mv1[:], stats[:]).then_inc(fs["resid"], 1)
                dve.wait_ge(fs["resid"], R + 5)
                nc.vector.tensor_scalar(rms_arg[:, 0:1], mv1[:, 0:1], mv1[:, 0:1], EPS_RMS, ALU.mult, ALU.add
                                        ).then_inc(fs["resid"], 1)
                dve.wait_ge(fs["resid"], R + 6)
                nc.vector.tensor_tensor(rms_arg[:, 1:2], rms_arg[:, 0:1], mv1[:, 1:2], ALU.add).then_inc(fs["resid"], 1)

            def dve_rms(dve, b, u):
                dve.wait_ge(fs["rstd"], b + 1)
                if later(b, 2):
                    dve.wait_ge(s_sc[u], 32 * (b - u))
                    dve.wait_ge(s_sh[u], 8 * (b - u))
                nc.vector.tensor_scalar(xn[:, u], r2[:], rms_inv[:], None, ALU.mult).then_inc(fs["xn"], 1)

            def dve_router_max(dve, b):
                dve.wait_ge(fs["logit"], b + 1)
                nc.vector.tensor_reduce(rneg[:], m_b[:, 0:E], AX.X, ALU.max, negate=True).then_inc(fs["rmax"], 1)

            def dve_choose(dve, b):
                R = 8 * b
                done = fs["route"]
                dve.wait_ge(fs["rexp"], b + 1)
                nc.vector.reciprocal(rrec[:], rsum[:]).then_inc(done, 1)
                dve.wait_ge(done, R + 1)
                nc.vector.tensor_scalar(both[:, 1], rexp[:], rrec[:], None, ALU.mult).then_inc(done, 1)
                dve.wait_ge(done, R + 2)
                nc.vector.tensor_tensor(biased[:], both[:, 1], bias_sb[:], ALU.add).then_inc(done, 1)
                dve.wait_ge(done, R + 3)
                hold_v()
                nc.vector.max(top8[:], biased[:]).then_inc(done, 1)
                dve.wait_ge(done, R + 4)
                hold_v()
                nc.vector.max_index(idx8[:], top8[:], biased[:]).then_inc(done, 1)
                dve.wait_ge(done, R + 5)
                nc.vector.tensor_copy(idxf[:], idx8[:, 0:TOPK]).then_inc(done, 1)
                dve.wait_ge(done, R + 6)
                nc.vector.tensor_tensor(oh[:], col["iota_e"].unsqueeze(1).to_broadcast([P, TOPK, E]),
                                        idxf[:].unsqueeze(2).to_broadcast([P, TOPK, E]), ALU.is_equal).then_inc(done, 1)
                dve.wait_ge(done, R + 7)
                with nc.allow_low_precision(reason="a sum of ones and zeros that is one or zero"):
                    nc.vector.tensor_reduce(mask16[:], oh[:].rearrange("p k e -> p e k"), AX.X, ALU.add
                                            ).then_inc(done, 1)

            def dve_slots(dve, b, u):
                R = 8 * b
                dve.wait_ge(fs["prefix"], b + 1)
                nc.vector.tensor_tensor(both[:, 0], m_b[:, 0:E], col["region"], ALU.add).then_inc(fs["slot"], 1)
                dve.wait_ge(fs["slot"], 3 * b + 1)
                dve.wait_ge(fs["route"], R + 8)
                nc.vector.tensor_tensor(prod[:], both[:].unsqueeze(2).to_broadcast([P, 2, TOPK, E]),
                                        oh[:].unsqueeze(1).to_broadcast([P, 2, TOPK, E]), ALU.mult).then_inc(fs["mix"], 1)
                nc.vector.tensor_tensor(counts[:], counts[:], mask16[:], ALU.add).then_inc(fs["mix"], 1)
                dve.wait_ge(fs["mix"], 8 * b + 2)
                nc.vector.tensor_reduce(picked[:], prod[:], AX.X, ALU.add).then_inc(fs["mix"], 1)
                nc.vector.tensor_copy(counts16[:], counts[:]).then_inc(fs["mix"], 1)
                dve.wait_ge(fs["mix"], 8 * b + 4)
                if later(b, 2):
                    dve.wait_ge(s_sc[u], 32 * (b - u))
                nc.vector.tensor_copy(islot[:, u], picked[:, 0]).then_inc(fs["slot"], 1)
                nc.vector.tensor_scalar(slots_all[:, b, :], picked[:, 0], 1.0, None, ALU.mult).then_inc(fs["slot"], 1)
                nc.vector.tensor_scalar(oh_all[:, b], oh[:], 1.0, None, ALU.mult).then_inc(fs["mix"], 1)
                nc.vector.tensor_reduce(wsum[:], picked[:, 1], AX.X, ALU.add).then_inc(fs["mix"], 1)
                dve.wait_ge(fs["mix"], 8 * b + 6)
                nc.vector.tensor_scalar(wmax[:], wsum[:], NORM_MIN, None, ALU.max).then_inc(fs["mix"], 1)
                dve.wait_ge(fs["mix"], 8 * b + 7)
                nc.vector.reciprocal(wrec[:], wmax[:]).then_inc(fs["mix"], 1)
                dve.wait_ge(fs["mix"], 8 * b + 8)
                nc.vector.tensor_scalar(rw_all[:, b, :], picked[:, 1], wrec[:], tanhs[:, 1:2], ALU.mult, ALU.mult
                                        ).then_inc(fs["weights"], 1)

            def pool_rotate(pool, b, r):
                pool.wait_ge(fs["cs"], 10 * b + 2 * r + 2)
                if r >= 2:
                    pool.wait_ge(fs["tp"], 5 * b + r - 1)
                elif later(b):
                    pool.wait_ge(fs["tp"], 5 * b + (0 if r == 0 else r - 1))
                nc.gpsimd.tensor_tensor(roped[:, r % 2], r_cos[:], r_sin[:], ALU.add).then_inc(fs["rope"], 1)

            def pool_rms(pool, b):
                pool.wait_ge(fs["resid"], 7 * b + 7)
                nc.gpsimd.tensor_tensor(rms_inv[:], rms_arg[:, 1:2], col["power"][:, 0:1], ALU.pow).then_inc(fs["rstd"], 1)

            def pool_scatter(pool, b, u):
                pool.wait_ge(fs["slot"], 3 * b + 2)
                pool.wait_ge(fs["xn"], b + 1)
                hold_p()
                for k in range(TOPK):
                    nc.gpsimd.indirect_dma_start(
                        out=x_rows, out_offset=bass.IndirectOffsetOnAxis(ap=islot[:, u, k:k + 1].bitcast(U32), axis=0),
                        in_=xn[:, u], in_offset=None).then_inc(s_sc[u], 16)

            def act_shared_rows(act, b, u):
                act.wait_ge(fs["xn"], b + 1)
                act.dma_start(x_rows[SHARED_ROW:SHARED_ROW + T].rearrange("(b p) h -> b p h", p=P)[b], xn[:, u]
                              ).then_inc(s_sh[u], 16)

            @block.tensor
            def _(pe):
                def body(b, u, prep=True, route=True):
                    pe_scores(pe, b, u, 0)
                    if prep:
                        pe_head_transpose(pe, b + 1)
                    pe_scores(pe, b, u, 1)
                    if prep:
                        pe_project(pe, b + 1, 0)
                        pe_project(pe, b + 1, 1)
                    pe_probs_transpose(pe, b, 0)
                    if route:
                        pe_router_transpose(pe, b - 1, 1 - u)
                    if prep:
                        pe_project(pe, b + 1, 2)
                    pe_weigh(pe, b, u, 0)
                    pe_scores(pe, b, u, 2)
                    if prep:
                        pe_chunk_transpose(pe, b + 1, 0)
                    pe_probs_transpose(pe, b, 1)
                    if route:
                        pe_logits(pe, b - 1)
                    if prep:
                        pe_project(pe, b + 1, 3)
                    pe_weigh(pe, b, u, 1)
                    pe_scores(pe, b, u, 3)
                    if prep:
                        pe_chunk_transpose(pe, b + 1, 1)
                    pe_probs_transpose(pe, b, 2)
                    if prep:
                        pe_project(pe, b + 1, 4)
                    pe_weigh(pe, b, u, 2)
                    if prep:
                        pe_chunk_transpose(pe, b + 1, 2)
                        pe_project(pe, b + 1, 5)
                    pe_probs_transpose(pe, b, 3)
                    if route:
                        pe_prefix(pe, b - 1)
                    if prep:
                        pe_chunk_transpose(pe, b + 1, 3)
                    pe_out(pe, b, 0, HQ - GQ)
                    pe_weigh(pe, b, u, 3)
                    if prep:
                        pe_chunk_transpose(pe, b + 1, 4)
                    pe_out(pe, b, HQ - GQ, HQ)

                pe.wait_ge(s_w, 4 * 16)
                pe.wait_ge(fs["init"], 3)
                pe_head_transpose(pe, 0)
                for c in range(6):
                    pe_project(pe, 0, c)
                    if c != 1:
                        pe_chunk_transpose(pe, 0, max(c - 1, 0))
                body(0, 0, route=False)
                body(1, 1)
                body(2, 0)
                with pe.Fori(0, (NB - 4) // 2) as i:
                    body(2 * i + 3, 1)
                    body(2 * i + 4, 0)
                body(NB - 1, 1, prep=False)
                pe_router_transpose(pe, NB - 1, 1)
                pe_logits(pe, NB - 1)
                pe_prefix(pe, NB - 1)

            @block.scalar
            def _(act):
                def body(b, u, prep=True, route=True):
                    act_exp(act, b, 0)
                    if prep:
                        act_head_transpose(act, b + 1)
                    act_exp(act, b, 1)
                    if prep:
                        act_values(act, b + 1, 1 - u)
                    act_probs(act, b, 0)
                    if route:
                        act_router_transpose(act, b - 1)
                        act_shared_rows(act, b - 1, 1 - u)
                    act_weighed(act, b, 0)
                    act_exp(act, b, 2)
                    if prep:
                        act_chunk(act, b + 1, 1 - u, 0)
                    act_probs(act, b, 1)
                    if route:
                        act_route(act, b - 1)
                    act_weighed(act, b, 1)
                    act_exp(act, b, 3)
                    if prep:
                        act_chunk(act, b + 1, 1 - u, 1)
                    act_probs(act, b, 2)
                    act_weighed(act, b, 2)
                    if prep:
                        act_chunk(act, b + 1, 1 - u, 2)
                    act_probs(act, b, 3)
                    if prep:
                        act_chunk(act, b + 1, 1 - u, 3)
                    act_weighed(act, b, 3)
                    if prep:
                        act_chunk(act, b + 1, 1 - u, 4)

                act_head_transpose(act, 0)
                act_chunk(act, 0, 0, 0)
                act_values(act, 0, 0)
                for r in range(1, 5):
                    act_chunk(act, 0, 0, r)
                body(0, 0, route=False)
                body(1, 1)
                body(2, 0)
                with act.Fori(0, (NB - 4) // 2) as i:
                    body(2 * i + 3, 1)
                    body(2 * i + 4, 0)
                body(NB - 1, 1, prep=False)
                act_router_transpose(act, NB - 1)
                act_shared_rows(act, NB - 1, 1)
                act_route(act, NB - 1)

            @block.vector
            def _(dve):
                def body(b, u, prep=True, route=True):
                    if prep:
                        dve_norm_rows(dve, b + 1)
                    dve_max(dve, b, 0)
                    if route:
                        dve_residual(dve, b - 1)
                    dve_max(dve, b, 1)
                    dve_normalize(dve, b, 0)
                    if route:
                        dve_rms(dve, b - 1, 1 - u)
                    if prep:
                        dve_rotate(dve, b + 1, 0)
                    dve_normalize(dve, b, 1)
                    if prep:
                        dve_rotate(dve, b + 1, 1)
                    dve_max(dve, b, 2)
                    if route:
                        dve_router_max(dve, b - 1)
                    if prep:
                        dve_rotate(dve, b + 1, 2)
                    dve_normalize(dve, b, 2)
                    dve_max(dve, b, 3)
                    if route:
                        dve_choose(dve, b - 1)
                    if prep:
                        dve_rotate(dve, b + 1, 3)
                    dve_normalize(dve, b, 3)
                    if route:
                        dve_slots(dve, b - 1, 1 - u)
                    if prep:
                        dve_rotate(dve, b + 1, 4)

                nc.vector.memset(counts[:], 0.0).then_inc(fs["init"], 1)
                nc.vector.memset(tick_v[:], 0.0).then_inc(fs["init"], 1)
                nc.vector.memset(counts16[:], 0.0).then_inc(fs["init"], 1)
                dve.wait_ge(fs["init"], 3)
                dve_norm_rows(dve, 0)
                for r in range(5):
                    dve_rotate(dve, 0, r)
                body(0, 0, route=False)
                body(1, 1)
                body(2, 0)
                with dve.Fori(0, (NB - 4) // 2) as i:
                    body(2 * i + 3, 1)
                    body(2 * i + 4, 0)
                body(NB - 1, 1, prep=False)
                dve_residual(dve, NB - 1)
                dve_rms(dve, NB - 1, 1)
                dve_router_max(dve, NB - 1)
                dve_choose(dve, NB - 1)
                dve_slots(dve, NB - 1, 1)

            @block.gpsimd
            def _(pool):
                def body(b, u, prep=True, route=True):
                    if route:
                        pool_rms(pool, b - 1)
                    if prep:
                        for r in range(5):
                            pool_rotate(pool, b + 1, r)
                    if route:
                        pool_scatter(pool, b - 1, 1 - u)

                nc.gpsimd.memset(tick_p[:], 0.0).then_inc(fs["pool_init"], 1)
                pool.wait_ge(fs["pool_init"], 1)
                for r in range(5):
                    pool_rotate(pool, 0, r)
                body(0, 0, route=False)
                body(1, 1)
                body(2, 0)
                with pool.Fori(0, (NB - 4) // 2) as i:
                    body(2 * i + 3, 1)
                    body(2 * i + 4, 0)
                body(NB - 1, 1, prep=False)
                pool_rms(pool, NB - 1)
                pool_scatter(pool, NB - 1, 1)
        nc.all_engine_barrier()

        tiles_i = sb("tiles_i", [P, 2, E], I32)
        tiles_e = sb("tiles_e", [P, E])
        ends = sb("ends", [P, E])
        delta = sb("delta", [P, E])
        below = sb("below", [P, 2, E])
        tile_of = sb("tile_of", [P, 4])
        tile_tab = sb("tile_tab", [1, 2, TILES], I32)
        pad_row = sb("pad_row", [P, E], I32)
        zeros = sb("zeros", [P, H])
        ypos = sb("ypos", [P, NB, TOPK], I32)
        yposf = sb("yposf", [P, NB * TOPK])
        moved = sb("moved", [P, NB * TOPK, E])

        xt_in = sb("xt_in", [P, 4, H])
        xt_t = sb("xt_t", [P, 2, KT, P])
        gate_act = sb("gate_act", [P, 2, I])
        hid = sb("hid", [P, 2, I])
        hid_t = sb("hid_t", [P, 2, P])
        y_out = sb("y_out", [P, 4, H])

        gath = sb("gath", [P, 2, TOPK, H])
        shared = sb("shared", [P, 2, H])
        idx = sb("idx", [P, 2, TOPK], I32)
        acc = sb("acc", [P, 2, H])

        bs = {n: sem("b_" + n) for n in ("plan", "count", "tab", "tabp", "iota", "zero", "pads", "xtp", "xt", "gu", "silu", "hid", "htp",
                                         "ht", "y", "yo", "ypos", "idx", "comb", "planp", "held")}
        s_xl = [sem(f"s_xl{i}") for i in range(4)]
        s_ys = [sem(f"s_ys{i}") for i in range(4)]
        s_g = [sem(f"s_g{i}") for i in range(2)]
        s_s = [sem(f"s_s{i}") for i in range(2)]
        s_o = [sem(f"s_o{i}") for i in range(2)]
        cnt_b = banks[:, 0]
        x_b, gu_b, h_b, y_b = (banks[:, 0], banks[:, 1]), (banks[:, 2], banks[:, 3]), (banks[:, 4], banks[:, 5]), \
            (banks[:, 6], banks[:, 7])
        LAST_SHARED = SHARED_ROW + T - P
        SKEW = 3

        with nc.Block() as block:
            def in_loop(s):
                return not isinstance(s, int)

            @block.sync
            def _(sp):
                load_expert_weights(sp, EARLY, E, wsem2)
                sp.wait_ge(bs["plan"], 8)
                sp.wait_ge(bs["zero"], 1)
                with sp.Fori(0, E) as e:
                    row = sp.value_load(pad_row[0:1, bass.ds(e, 1)], min_val=0, max_val=SHARED_ROW - P)
                    sp.dma_start(x_rows[bass.ds(row, P), :], zeros[:]).then_inc(bs["pads"], 16)

            @block.gpsimd
            def _(pool):
                nc.gpsimd.memset(zeros[:], 0.0).then_inc(bs["zero"], 1)
                nc.gpsimd.iota(tile_tab[0:1, 0, 0:NB], pattern=[[0, NB]], base=E, channel_multiplier=0
                               ).then_inc(bs["iota"], 1)
                for t in range(NB):
                    nc.gpsimd.memset(tile_tab[0:1, 1, t:t + 1], SHARED_ROW + t * P).then_inc(bs["iota"], 1)
                pool.wait_ge(bs["iota"], NB + 1)
                pool.wait_ge(bs["tab"], 1)
                for u in range(2):
                    pool.wait_ge(s_sh[u], 8 * NB)

                def load_tile(s, i):
                    row = pool.value_load(tile_tab[0:1, 1, bass.ds(s, 1)] if in_loop(s) else tile_tab[0:1, 1, s:s + 1],
                                          min_val=0, max_val=LAST_SHARED)
                    if in_loop(s) or s >= 4:
                        pool.wait_ge(bs["xtp"], s - 3)
                    pool.dma_start(xt_in[:, i], x_rows[bass.ds(row, P), :]).then_inc(s_xl[i], 16)

                for s in range(4):
                    load_tile(s, s)
                with pool.Fori(0, NB // 4 - 1) as i:
                    for j in range(4):
                        load_tile(4 * i + 4 + j, j)
                for u in range(2):
                    pool.wait_ge(s_sc[u], 32 * NB)
                pool.wait_ge(bs["pads"], 16 * E)
                with pool.Fori(0, ROUTED_TILES // 4) as i:
                    for j in range(4):
                        load_tile(4 * i + NB + j, j)

                for i in range(4):
                    pool.wait_ge(s_ys[i], 16 * (TILES // 4))

                def gather(b, u):
                    pool.wait_ge(bs["idx"], b + 1)
                    if in_loop(b) or b >= 2:
                        pool.wait_ge(bs["comb"], 5 * b - 5)
                        pool.wait_ge(bs["held"], b - 1)
                    hold_p(u).then_inc(bs["held"], 1)
                    for k in range(TOPK):
                        nc.gpsimd.indirect_dma_start(
                            out=gath[:, u, k], out_offset=None, in_=y_rows,
                            in_offset=bass.IndirectOffsetOnAxis(ap=idx[:, u, k:k + 1].bitcast(U32), axis=0)
                        ).then_inc(s_g[u], 16)

                gather(0, 0)
                gather(1, 1)
                with pool.Fori(0, (NB - 2) // 2) as i:
                    gather(2 * i + 2, 0)
                    gather(2 * i + 3, 1)

            @block.tensor
            def _(pe):
                nc.tensor.matmul(cnt_b[:, 0:E], ones16[:], counts16[:], start=True, stop=True).then_inc(bs["count"], 1)
                pe.wait_ge(bs["planp"], 4)
                for n in range(2):
                    last = nc.tensor.matmul(banks[0:1, 1, n * P:(n + 1) * P], tile_of[:, 2 + n:3 + n], ident,
                                            start=True, stop=True)
                last.then_inc(bs["tabp"], 1)
                pe.wait_ge(bs["tab"], 1)
                pe.wait_ge(bs["iota"], NB + 1)
                pe.wait_ge(wsem, 6 * 16)

                def expert_of(s):
                    at = tile_tab[0:1, 0, bass.ds(s, 1)] if in_loop(s) else tile_tab[0:1, 0, s:s + 1]
                    return pe.value_load(at, min_val=0, max_val=E)

                def step(s, j, lo=0, hi=TILES):
                    if in_loop(s) or s < TILES:
                        pe.wait_ge(s_xl[j], 4 * (s - j) + 16)
                        if in_loop(s) or s >= 2:
                            pe.wait_ge(bs["xt"], s - 1)
                        for t in range(KT):
                            last = nc.tensor.transpose(x_b[j % 2][:, t * P:(t + 1) * P], xt_in[:, j, t * P:(t + 1) * P], ident)
                        last.then_inc(bs["xtp"], 1)
                    if in_loop(s) or 1 <= s < TILES + 1:
                        e = expert_of(s - 1)
                        pe.wait_ge(bs["xt"], s)
                        if in_loop(s) or s >= 3:
                            pe.wait_ge(bs["hid"], s - 2)
                        for t in range(KT):
                            last = nc.tensor.matmul(gu_b[(j - 1) % 2][:, 0:2 * I], xt_t[:, (j - 1) % 2, t],
                                                    gu[:, bass.ds(e, 1), t, :].rearrange("p a n -> p (a n)"),
                                                    start=(t == 0), stop=(t == KT - 1))
                        last.then_inc(bs["gu"], 1)
                    if in_loop(s) or 2 <= s < TILES + 2:
                        pe.wait_ge(bs["hid"], s - 1)
                        if in_loop(s) or s >= 4:
                            pe.wait_ge(bs["ht"], s - 3)
                        nc.tensor.transpose(h_b[j % 2][:, 0:P], hid[:, j % 2], ident).then_inc(bs["htp"], 1)
                    if in_loop(s) or 3 <= s:
                        e = expert_of(s - 3)
                        pe.wait_ge(bs["ht"], s - 2)
                        if in_loop(s) or s >= 5:
                            pe.wait_ge(bs["yo"], s - 4)
                        nc.tensor.matmul(y_b[(j - 1) % 2][:, 0:H], hid_t[:, (j - 1) % 2],
                                         dn[:, bass.ds(e, 1), :].rearrange("p a n -> p (a n)"), start=True, stop=True
                                         ).then_inc(bs["y"], 1)

                for s in range(8):
                    step(s, s % 4)
                with pe.Fori(0, (NB + EARLY) // 4 - 2) as i:
                    for j in range(4):
                        step(4 * i + 8 + j, j)
                pe.wait_ge(wsem2, 32)
                with pe.Fori(0, (TILES - NB - EARLY) // 4) as i:
                    for j in range(4):
                        step(4 * i + NB + EARLY + j, j)
                for s in range(TILES, TILES + SKEW):
                    step(s, s % 4)

            @block.scalar
            def _(act):
                def step(s, j):
                    if in_loop(s) or 1 <= s < TILES + 1:
                        act.wait_ge(bs["gu"], s)
                        if in_loop(s) or s >= 3:
                            act.wait_ge(bs["hid"], s - 2)
                        nc.scalar.activation(gate_act[:, (j - 1) % 2], gu_b[(j - 1) % 2][:, 0:I], ACT.Silu
                                             ).then_inc(bs["silu"], 1)
                    if in_loop(s) or 2 <= s < TILES + 2:
                        act.wait_ge(bs["htp"], s - 1)
                        if in_loop(s) or s >= 4:
                            act.wait_ge(bs["y"], s - 3)
                        nc.scalar.copy(hid_t[:, j % 2], h_b[j % 2][:, 0:P]).then_inc(bs["ht"], 1)
                    if in_loop(s) or 3 <= s:
                        i = (j - 3) % 4
                        act.wait_ge(bs["y"], s - 2)
                        if in_loop(s) or s >= 7:
                            act.wait_ge(s_ys[i], 4 * (s - 3 - i))
                        nc.scalar.copy(y_out[:, i], y_b[(j - 1) % 2][:, 0:H]).then_inc(bs["yo"], 1)
                        at = y_tiles[s - 3]
                        act.wait_ge(bs["yo"], s - 2)
                        act.dma_start(at, y_out[:, i]).then_inc(s_ys[i], 16)

                y_tiles = y_rows.rearrange("(t p) h -> t p h", p=P)
                for s in range(8):
                    step(s, s % 4)
                with act.Fori(0, TILES // 4 - 2) as i:
                    for j in range(4):
                        step(4 * i + 8 + j, j)
                for s in range(TILES, TILES + SKEW):
                    step(s, s % 4)

                for i in range(4):
                    act.wait_ge(s_ys[i], 16 * (TILES // 4))

                def move(b, u, ahead=True):
                    act.wait_ge(bs["comb"], 5 * b + 5)
                    act.dma_start(out[b], acc[:, u]).then_inc(s_o[u], 16)
                    if ahead:
                        act.dma_start(shared[:, u], y_tiles[b + 2]).then_inc(s_s[u], 16)

                act.dma_start(shared[:, 0], y_tiles[0]).then_inc(s_s[0], 16)
                act.dma_start(shared[:, 1], y_tiles[1]).then_inc(s_s[1], 16)
                with act.Fori(0, (NB - 2) // 2) as i:
                    move(2 * i, 0)
                    move(2 * i + 1, 1)
                move(NB - 2, 0, ahead=False)
                move(NB - 1, 1, ahead=False)
                for u in range(2):
                    act.wait_ge(s_o[u], 16 * (NB // 2))

            @block.vector
            def _(dve):
                plan, planp = bs["plan"], bs["planp"]
                dve.wait_ge(bs["count"], 1)
                nc.vector.tensor_scalar(tiles_i[:, 0], cnt_b[:, 0:E], float(P - 1), None, ALU.add).then_inc(plan, 1)
                nc.vector.tensor_tensor(pad_row[:], cnt_b[:, 0:E], col["region"], ALU.add).then_inc(plan, 1)
                dve.wait_ge(plan, 1)
                nc.vector.tensor_single_scalar(tiles_i[:, 1], tiles_i[:, 0], 7, ALU.arith_shift_right).then_inc(plan, 1)
                dve.wait_ge(plan, 3)
                nc.vector.tensor_copy(tiles_e[:], tiles_i[:, 1]).then_inc(plan, 1)
                dve.wait_ge(plan, 4)
                nc.vector.tensor_tensor_scan(ends[:], tiles_e[:], tiles_e[:], 0.0, ALU.add, ALU.bypass).then_inc(plan, 1)
                dve.wait_ge(plan, 5)
                nc.vector.tensor_scalar(below[:, 0], ends[:], col["tile_no"], None, ALU.is_le).then_inc(plan, 1)
                nc.vector.tensor_tensor(delta[:], ends[:], tiles_e[:], ALU.subtract).then_inc(plan, 1)
                dve.wait_ge(plan, 7)
                nc.vector.tensor_tensor(below[:, 1], below[:, 0], tiles_e[:], ALU.mult).then_inc(plan, 1)
                dve.wait_ge(plan, 8)
                nc.vector.tensor_reduce(tile_of[:, 0:2], below[:], AX.X, ALU.add).then_inc(planp, 1)
                dve.wait_ge(planp, 1)
                nc.vector.tensor_tensor(tile_of[:, 1:2], col["tile_no"], tile_of[:, 1:2], ALU.subtract).then_inc(planp, 1)
                nc.vector.tensor_scalar(tile_of[:, 2:3], tile_of[:, 0:1], float(E - 1), None, ALU.min).then_inc(planp, 1)
                dve.wait_ge(planp, 3)
                nc.vector.tensor_scalar(tile_of[:, 0:1], tile_of[:, 0:1], float(REGION), None, ALU.mult
                                        ).then_inc(bs["ypos"], 1)
                nc.vector.tensor_scalar(tile_of[:, 1:2], tile_of[:, 1:2], float(P), None, ALU.mult
                                        ).then_inc(bs["ypos"], 1)
                dve.wait_ge(bs["ypos"], 2)
                nc.vector.tensor_scalar(tile_of[:, 3:4], tile_of[:, 0:1], tile_of[:, 1:2], float(LAST_SHARED), ALU.add,
                                        ALU.min).then_inc(planp, 1)
                dve.wait_ge(bs["tabp"], 1)
                nc.vector.tensor_copy(tile_tab[0:1, :, NB:TILES],
                                      banks[0:1, 1, 0:2 * P].rearrange("p (a t) -> p a t", a=2)[:, :, 0:ROUTED_TILES]
                                      ).then_inc(bs["tab"], 1)
                nc.vector.tensor_scalar(delta[:], delta[:], float(P), float(NB * P), ALU.mult, ALU.add
                                        ).then_inc(bs["ypos"], 1)
                dve.wait_ge(bs["ypos"], 3)
                nc.vector.tensor_tensor(delta[:], delta[:], col["region"], ALU.subtract).then_inc(bs["ypos"], 1)

                def positions():
                    dve.wait_ge(bs["ypos"], 4)
                    nc.vector.tensor_tensor(moved[:], oh_all[:].rearrange("p b k e -> p (b k) e"),
                                            delta[:].unsqueeze(1).to_broadcast([P, NB * TOPK, E]), ALU.mult
                                            ).then_inc(bs["ypos"], 1)
                    dve.wait_ge(bs["ypos"], 5)
                    nc.vector.tensor_reduce(yposf[:], moved[:], AX.X, ALU.add).then_inc(bs["ypos"], 1)
                    dve.wait_ge(bs["ypos"], 6)
                    nc.vector.tensor_tensor(ypos[:].rearrange("p b k -> p (b k)"), yposf[:],
                                            slots_all[:].rearrange("p b k -> p (b k)"), ALU.add).then_inc(bs["ypos"], 1)

                def step(s, j):
                    if in_loop(s) or s < TILES:
                        dve.wait_ge(bs["xtp"], s + 1)
                        if in_loop(s) or s >= 2:
                            dve.wait_ge(bs["gu"], s - 1)
                        nc.vector.tensor_tensor(xt_t[:, j % 2], x_b[j % 2][:, 0:H].rearrange("p (t n) -> p t n", t=KT),
                                                lnw[:, 1].unsqueeze(2).to_broadcast([P, KT, P]), ALU.mult
                                                ).then_inc(bs["xt"], 1)
                    if in_loop(s) or 1 <= s < TILES + 1:
                        dve.wait_ge(bs["silu"], s)
                        if in_loop(s) or s >= 3:
                            dve.wait_ge(bs["htp"], s - 2)
                        nc.vector.tensor_tensor(hid[:, (j - 1) % 2], gu_b[(j - 1) % 2][:, I:2 * I], gate_act[:, (j - 1) % 2],
                                                ALU.mult).then_inc(bs["hid"], 1)

                for s in range(8):
                    step(s, s % 4)
                positions()
                with dve.Fori(0, TILES // 4 - 2) as i:
                    for j in range(4):
                        step(4 * i + 8 + j, j)
                step(TILES, 0)

                def indices(b, u):
                    if in_loop(b) or b >= 2:
                        dve.wait_ge(s_g[u], 32 * (b - u))
                    nc.vector.tensor_scalar(idx[:, u], ypos[:, b, :], 1.0, None, ALU.mult).then_inc(bs["idx"], 1)

                def combine(b, u, ahead=True):
                    dve.wait_ge(s_s[u], 8 * (b - u) + 16)
                    if in_loop(b) or b >= 2:
                        dve.wait_ge(s_o[u], 8 * (b - u))
                    nc.vector.scalar_tensor_tensor(acc[:, u], shared[:, u], tanhs[:, 1:2], x1[:, b, :], ALU.mult, ALU.add
                                                   ).then_inc(bs["comb"], 1)
                    dve.wait_ge(s_g[u], 32 * (b - u) + 64)
                    for k in range(TOPK):
                        dve.wait_ge(bs["comb"], 5 * b + k + 1)
                        nc.vector.scalar_tensor_tensor(acc[:, u], gath[:, u, k], rw_all[:, b, k:k + 1], acc[:, u], ALU.mult,
                                                       ALU.add).then_inc(bs["comb"], 1)
                    if ahead:
                        indices(b + 2, u)

                dve.wait_ge(bs["ypos"], 7)
                indices(0, 0)
                indices(1, 1)
                combine(0, 0)
                combine(1, 1)
                with dve.Fori(0, (NB - 4) // 2) as i:
                    combine(2 * i + 2, 0)
                    combine(2 * i + 3, 1)
                combine(NB - 2, 0, ahead=False)
                combine(NB - 1, 1, ahead=False)


def kernel(x, ctx_2048, g_xattn, g_ffn, L0_xattn_gamma, L0_ffn_ln1_w, L0_ffn_ln2_w, L0_ffn_wq, L0_ffn_wk, L0_ffn_wv,
           L0_ffn_wo, L0_ffn_gate_w, L0_ffn_bias_e, L0_ffn_weg, L0_ffn_weu, L0_ffn_wed, L0_ffn_wsg, L0_ffn_wsu,
           L0_ffn_wsd):
    import concourse.bacc as bacc
    from concourse.bass_utils import run_bass_kernel_spmd

    def by_channel(w):
        return np.asarray(w).reshape(KT, P).T

    arrays = {
        "x": x, "ctx": ctx_2048, "g_xattn": g_xattn, "g_ffn": g_ffn, "gamma": np.asarray(L0_xattn_gamma).reshape(1),
        "ln1_w": by_channel(L0_ffn_ln1_w), "ln2_w": by_channel(L0_ffn_ln2_w), "wq": L0_ffn_wq, "wk": L0_ffn_wk,
        "wv": L0_ffn_wv, "wo": L0_ffn_wo,
        "gate_wt": np.asarray(L0_ffn_gate_w).T.reshape(KT, P, E).transpose(1, 0, 2), "bias_e": L0_ffn_bias_e,
        "weg": L0_ffn_weg, "weu": L0_ffn_weu, "wed": L0_ffn_wed, "wsg": L0_ffn_wsg, "wsu": L0_ffn_wsu,
        "wsd": L0_ffn_wsd, "consts": constant_table(),
    }
    nc = bacc.Bacc("TRN2", target_bir_lowering=False, num_devices=1)
    feeds, args = {}, []
    for name, a in arrays.items():
        a = np.ascontiguousarray(a)
        feeds[f"in_{name}"] = a
        args.append(nc.dram_tensor(f"in_{name}", a.shape, mybir.dt.from_np(a.dtype), kind="ExternalInput").ap())
    out = nc.dram_tensor("out_x", (NB, S, H), F32, kind="ExternalOutput").ap()
    build(nc, *args, out)
    r = run_bass_kernel_spmd(nc, [feeds], core_ids=[0])
    return r.results[0]["out_x"]
```

```python
from contextlib import ExitStack

import numpy as np

import concourse.bass as bass
from concourse import mybir

F32 = mybir.dt.float32
BF16 = mybir.dt.bfloat16
I32 = mybir.dt.int32
U32 = mybir.dt.uint32
ALU = mybir.AluOpType
ACT = mybir.ActivationFunctionType
AX = mybir.AxisListType

P = 128
NB, S, H = 16, 128, 256
KT = H // P
XH, XD, XL = 8, 16, 256
QB = NB // 4
RING = 4
NPAR = 2
HQ, HKV, D = 16, 4, 128
GQ = HQ // HKV
E, TOPK, I = 32, 4, 128
EPS_LN, EPS_RMS, NORM_MIN = 1e-5, 1e-6, 1e-12
THETA = 10000.0
MASKED = -1e30

T = NB * S
REGION = T + P
SHARED_ROW = E * REGION
X_ROWS = SHARED_ROW + T
ROUTED_TILES = (T * TOPK - E) // P + E + 1
TILES = NB + ROUTED_TILES
Y_ROWS = TILES * P

COLS, _at = {}, 0
for _name, _n in (("ident", P), ("before", P), ("causal", P), ("q_cos", D), ("q_sin", D), ("k_cos", D),
                  ("k_sin", D), ("head_row", XH), ("ones_mask", NPAR * 32),
                  ("iota_e", E), ("region", E), ("power", 2 * NB), ("tile_no", 1), ("tile_no_row", NB)):
    COLS[_name] = (_at, _at + _n)
    _at += _n
NCONST = _at



BEFORE = 4
SKEW = 3
WORDS = (BEFORE + TILES + SKEW + 3) // 4
EBITS = 6


def constant_table():
    t = np.zeros((P, NCONST), np.float32)

    def put(name, value):
        a, b = COLS[name]
        t[:, a:b] = value

    p = np.arange(P)
    put("ident", np.eye(P))
    put("before", p[:, None] < p[None, :])
    put("causal", np.where(p[None, :] <= p[:, None], 0.0, MASKED))
    inv = (1.0 / THETA ** (np.arange(0, D, 2, dtype=np.float32) / np.float32(D))).astype(np.float32)
    ang = np.arange(S, dtype=np.float32)[:, None] * inv[None, :]
    cos = np.repeat(np.cos(ang), 2, axis=1)
    sin = np.repeat(np.sin(ang), 2, axis=1)
    sin[:, 0::2] *= -1
    scale = 1.0 / np.sqrt(np.float32(D))
    put("q_cos", cos * scale)
    put("q_sin", sin * scale)
    put("k_cos", cos)
    put("k_sin", sin)
    put("head_row", p[:, None] % XH == np.arange(XH)[None, :])
    half = np.arange(32) // XD
    put("ones_mask", np.concatenate([half == 0, half == 1])[None, :])
    put("iota_e", np.arange(E)[None, :])
    put("region", np.arange(E)[None, :] * REGION)
    put("power", -0.5)
    put("tile_no", p[:, None])
    put("tile_no_row", np.arange(NB)[None, :])
    return t


def later(b, n=1):
    return not isinstance(b, int) or b >= n


def build(nc, x, ctx_in, g_xattn, g_ffn, gamma, ln1_w, ln2_w, wq, wk, wv, wo, gate_wt, bias_e,
          weg, weu, wed, wsg, wsu, wsd, consts, out):
    x_rows = nc.dram_tensor("x_rows", (X_ROWS, H), F32, kind="Internal").ap()
    y_rows = nc.dram_tensor("y_rows", (Y_ROWS, H), F32, kind="Internal").ap()

    q_dram = nc.dram_tensor("q_dram", (RING, 3, XD, XH, XL), BF16, kind="Internal").ap()
    k_dram = nc.dram_tensor("k_dram", (RING, 3, XD, XH, XL), BF16, kind="Internal").ap()

    with ExitStack() as stack:
        def sb(name, shape, dt=F32):
            return stack.enter_context(nc.sbuf_tensor(name, shape, dt))

        def bank(name, n=1):
            return stack.enter_context(nc.psum_tensor(name, [P, n, 512], F32))

        def sem(name):
            return stack.enter_context(nc.semaphore(name))

        tab = sb("tab", [P, NCONST])
        col = {k: tab[:, a:b] for k, (a, b) in COLS.items()}
        ident = col["ident"]
        before16 = sb("before16", [P, P], BF16)
        causal16 = sb("causal16", [P, P], BF16)
        ident16 = sb("ident16", [P, P], BF16)
        ones16 = sb("ones16", [P, P], BF16)
        gates = sb("gates", [P, 3])
        tanhs = sb("tanhs", [P, 2])
        tgx = sb("tgx", [P, 1])
        lnw = sb("lnw", [P, 2, KT])
        bias_sb = sb("bias_sb", [P, E])
        x1 = sb("x1", [P, NB, H])
        stats = sb("stats", [P, 6])
        mv1 = sb("mv1", [P, 2])
        mv = sb("mv", [P, NB, 2])
        arg = sb("arg", [P, 2, NB])
        inv = sb("inv", [P, 2, NB])
        wq_sb = sb("wq_sb", [P, KT, HQ * D])
        wk_sb = sb("wk_sb", [P, KT, HKV * D])
        wv_sb = sb("wv_sb", [P, KT, HKV * D])
        gate_sb = sb("gate_sb", [P, KT, E])

        banks = bank("banks", 8)

        s_tab = sem("s_tab")
        s_in = sem("s_in")
        s_x = [sem(f"s_x{i}") for i in range(4)]
        s_w = sem("s_w")

        with ExitStack() as px:
            def xsb(name, shape, dt=F32):
                return px.enter_context(nc.sbuf_tensor(name, shape, dt))

            ctx_sb = xsb("ctx_sb", [P, RING, XL])
            q_norm = xsb("q_norm", [P, 2, XL])
            x_zero = xsb("x_zero", [P, XL])
            q_rest = xsb("q_rest", [P, XL])
            k_rest = xsb("k_rest", [P, XL])
            q_parts = xsb("q_parts", [P, 2, 3, XL], BF16)
            k_parts = xsb("k_parts", [P, RING, 3, XL], BF16)
            q_stack = xsb("q_stack", [P, RING, XH, XL], BF16)
            k_stack = xsb("k_stack", [P, RING, XH, XL], BF16)
            negmax = xsb("negmax", [P, 2, XH])
            max_rest = xsb("max_rest", [P, 2, XH])
            max_parts = xsb("max_parts", [P, 2, 3, XH], BF16)
            max_t = xsb("max_t", [3 * XH, XL], BF16)
            head_sel = xsb("head_sel", [3 * XH, XH, P], BF16)
            v_t = xsb("v_t", [P, 2, NPAR, 2, P])
            ones_par = xsb("ones_par", [P, NPAR, 32])
            probs = xsb("probs", [P, 4, 2, 2, XL])
            den_r = xsb("den_r", [P, XL])
            ret = xsb("ret", [P, XL])
            ret2 = xsb("ret2", [P, XL])

            xs = {n: sem("x_" + n) for n in (
                "setup", "tanh", "st", "mv", "arg", "inv", "q", "q_split", "k_split", "scores", "max", "max_split",
                "mtp", "mt", "tscores", "exp", "pv", "vtp", "vt", "rec", "ret", "x1", "st2", "mv2", "agg2", "arg2",
                "inv2", "cast")}
            s_ctx = [sem(f"s_ctx{i}") for i in range(RING)]
            s_st = [sem(f"s_st{i}") for i in range(RING)]
            s_ld = [sem(f"s_ld{i}") for i in range(RING)]
            block = px.enter_context(nc.Block())

            sc_b, t_b, pv_b = (banks[:, 0], banks[:, 1]), (banks[:, 2:4], banks[:, 4:6]), banks[:, 6]
            mt_b, vt_b = banks[0:3 * XH, 7, 0:XL], banks[:, 7, XL:2 * XL]

            def heads_of(unit):
                return [2 * (2 * (unit % 2) + j) + unit // 2 for j in range(2)]

            def store_parts(eng, b, j):
                if later(b, RING):
                    eng.wait_ge(s_ld[j], 24 * (b - j))
                for split, parts, dram in ((xs["q_split"], q_parts[:, j % 2], q_dram),
                                           (xs["k_split"], k_parts[:, j], k_dram)):
                    eng.wait_ge(split, 4 * b + 4)
                    for t in range(3):
                        eng.dma_start(dram[j, t].rearrange("i h l -> h i l"), parts[:, t]).then_inc(s_st[j], 16)

            def load_stacks(eng, b, j):
                eng.wait_ge(s_st[j], 24 * (b - j) + 96)
                if later(b, RING):
                    eng.wait_ge(xs["tscores"], 4 * b - 12)
                for t in range(3):
                    n = 3 if t < 2 else 2
                    at = 3 * XD * t
                    eng.dma_start(q_stack[at:at + n * XD, j], q_dram[j, 0:n].rearrange("t i h l -> (t i) (h l)")
                                  ).then_inc(s_ld[j], 16)
                    eng.dma_start(k_stack[at:at + n * XD, j], k_dram[j, t:t + 1].rearrange("t i h l -> t i (h l)")
                                  .to_broadcast([n, XD, XH * XL])).then_inc(s_ld[j], 16)

            @block.sync
            def _(sp):
                sp.dma_start(x1[:, 0:QB, :], x[0:QB].rearrange("b s h -> s b h")).then_inc(s_x[0], 16)
                for i in range(1, 4):
                    sp.dma_start(x1[:, QB * i:QB * (i + 1), :],
                                 x[QB * i:QB * (i + 1)].rearrange("b s h -> s b h")).then_inc(s_x[i], 16)

                for b in range(RING - 1):
                    store_parts(sp, b, b)
                    load_stacks(sp, b, b)
                sp.dma_start(gate_sb[:], gate_wt).then_inc(s_w, 16)
                for w_sb, w in ((wk_sb, wk), (wv_sb, wv), (wq_sb, wq)):
                    sp.dma_start(w_sb[:], w.rearrange("(t p) n -> p t n", p=P)).then_inc(s_w, 16)

            def inverse_roots(pool, arg_sem, n, first, size, count, done):
                pool.wait_ge(arg_sem, n)
                nc.gpsimd.tensor_tensor(inv[:, 0:count, first:first + size], arg[:, 0:count, first:first + size],
                                        col["power"].rearrange("p (a b) -> p a b", a=2)[:, 0:count, 0:size], ALU.pow
                                        ).then_inc(done, 1)

            def split(pool, b, src, parts, rest, done):
                if later(b):
                    pool.wait_ge(done, 4 * b)
                nc.gpsimd.tensor_tensor(parts[:, 0], src, x_zero[:], ALU.add).then_inc(done, 1)
                pool.wait_ge(done, 4 * b + 1)
                nc.gpsimd.tensor_tensor(rest[:], src, parts[:, 0], ALU.subtract).then_inc(done, 1)
                pool.wait_ge(done, 4 * b + 2)
                nc.gpsimd.tensor_tensor(parts[:, 1], rest[:], x_zero[:], ALU.add).then_inc(done, 1)
                pool.wait_ge(done, 4 * b + 3)
                nc.gpsimd.tensor_tensor(parts[:, 2], rest[:], parts[:, 1], ALU.subtract).then_inc(done, 1)

            @block.gpsimd
            def _(pool):
                nc.gpsimd.memset(x_zero[:], 0.0).then_inc(xs["setup"], 1)
                pool.wait_ge(xs["setup"], 1)
                pool.wait_ge(s_tab, 16)
                inverse_roots(pool, xs["arg"], 1, 0, QB, 1, xs["inv"])

                def parts(b, j):
                    u = j % 2
                    if later(b, 2):
                        pool.wait_ge(s_st[(j - 2) % RING], 24 * (b - 2 - (j - 2) % RING) + 96)
                    pool.wait_ge(xs["q"], b + 1)
                    split(pool, b, q_norm[:, u], q_parts[:, u], q_rest, xs["q_split"])
                    pool.wait_ge(s_ctx[j], 4 * (b - j) + 16)
                    if later(b, RING):
                        pool.wait_ge(xs["vtp"], b - RING + 1)
                    split(pool, b, ctx_sb[:, j], k_parts[:, j], k_rest, xs["k_split"])

                parts(0, 0)
                nc.gpsimd.memset(v_t[:], 0.0).then_inc(xs["setup"], 1)
                nc.gpsimd.memset(ones16[:], 1.0).then_inc(xs["setup"], 1)
                parts(1, 1)
                parts(2, 2)
                for g in range(1, NB // QB):
                    inverse_roots(pool, xs["arg"], g + 1, QB * g, QB, 1, xs["inv"])
                parts(3, 3)
                with pool.Fori(0, NB // RING - 1) as i:
                    for j in range(RING):
                        parts(RING * i + RING + j, j)
                inverse_roots(pool, xs["arg2"], 2, 0, NB - 4, 2, xs["inv2"])
                inverse_roots(pool, xs["arg2"], 4, NB - 4, 4, 2, xs["inv2"])

            def queries(dve, b, u):
                if later(b, 2):
                    dve.wait_ge(xs["q_split"], 4 * b - 4)
                nc.vector.tensor_scalar(q_norm[:, u], x1[:, b, :], mv[:, b, 0:1], inv[:, 0, bass.ds(b, 1)],
                                        ALU.subtract, ALU.mult).then_inc(xs["q"], 1)

            def maximum(dve, b, h):
                dve.wait_ge(xs["scores"], XH * b + h + 1)
                if h == 0 and later(b):
                    dve.wait_ge(xs["max_split"], 4 * b)
                nc.vector.tensor_reduce(negmax[:, :, h:h + 1].rearrange("p t a -> p (t a)"),
                                        sc_b[h % 2].rearrange("p (t l) -> p t l", t=2), AX.X, ALU.max, negate=True
                                        ).then_inc(xs["max"], 1)

            def split_maxima(dve, b):
                done = xs["max_split"]
                dve.wait_ge(xs["max"], XH * b + XH)
                if later(b):
                    dve.wait_ge(xs["mtp"], b)
                nc.vector.tensor_copy(max_parts[:, :, 0], negmax[:]).then_inc(done, 1)
                dve.wait_ge(done, 4 * b + 1)
                nc.vector.tensor_tensor(max_rest[:], negmax[:], max_parts[:, :, 0], ALU.subtract).then_inc(done, 1)
                dve.wait_ge(done, 4 * b + 2)
                nc.vector.tensor_copy(max_parts[:, :, 1], max_rest[:]).then_inc(done, 1)
                dve.wait_ge(done, 4 * b + 3)
                nc.vector.tensor_tensor(max_parts[:, :, 2], max_rest[:], max_parts[:, :, 1], ALU.subtract
                                        ).then_inc(done, 1)

            def keep_maxima(dve, b):
                dve.wait_ge(xs["mtp"], b + 1)
                if later(b):
                    dve.wait_ge(xs["tscores"], 4 * b)
                nc.vector.tensor_copy(max_t[:], mt_b).then_inc(xs["mt"], 1)

            def divide(dve, b):
                dve.wait_ge(xs["pv"], 2 * b + 2)
                nc.vector.reciprocal(den_r[:], pv_b[:, XL:2 * XL]).then_inc(xs["rec"], 1)
                dve.wait_ge(xs["rec"], b + 1)
                nc.vector.tensor_tensor(ret[:], pv_b[:, 0:XL], den_r[:], ALU.mult).then_inc(xs["ret"], 1)

            def residual(dve, b):
                dve.wait_ge(xs["ret"], b + 1)
                nc.vector.scalar_tensor_tensor(ret2[:], ret[:], tgx[:], x1[:, b, :], ALU.mult, ALU.add
                                               ).then_inc(xs["x1"], 1)
                dve.wait_ge(xs["x1"], b + 1)
                nc.vector.bn_stats(stats[:], ret2[:]).then_inc(xs["st2"], 1)
                dve.wait_ge(xs["st2"], b + 1)
                nc.vector.tensor_scalar(x1[:, b, :], ret2[:], 1.0, None, ALU.mult)
                nc.vector.bn_aggr(mv1[:], stats[:]).then_inc(xs["agg2"], 1)
                dve.wait_ge(xs["agg2"], b + 1)
                nc.vector.tensor_scalar(mv[:, b, :], mv1[:], 1.0, None, ALU.mult).then_inc(xs["mv2"], 1)

            @block.vector
            def _(dve):
                for g in range(NB // QB):
                    dve.wait_ge(s_x[g], 16)
                    for b in range(QB * g, QB * (g + 1)):
                        if b:
                            dve.wait_ge(xs["mv"], b)
                        nc.vector.bn_stats(stats[:], x1[:, b, :]).then_inc(xs["st"], 1)
                        dve.wait_ge(xs["st"], b + 1)
                        nc.vector.bn_aggr(mv[:, b, :], stats[:]).then_inc(xs["mv"], 1)
                    dve.wait_ge(xs["mv"], QB * (g + 1))
                    nc.vector.tensor_scalar_add(arg[:, 0, QB * g:QB * (g + 1)], mv[:, QB * g:QB * (g + 1), 1], EPS_LN
                                                ).then_inc(xs["arg"], 1)
                    if g == 0:
                        dve.wait_ge(xs["inv"], 1)
                        for b in range(RING - 1):
                            queries(dve, b, b % 2)
                dve.wait_ge(s_tab, 16)
                dve.wait_ge(s_in, 6 * 16)
                nc.vector.tensor_copy(before16[:], col["before"]).then_inc(xs["cast"], 1)
                nc.vector.tensor_copy(causal16[:], col["causal"]).then_inc(xs["cast"], 1)
                nc.vector.tensor_copy(ident16[:], ident).then_inc(xs["cast"], 1)
                nc.vector.tensor_copy(ones_par[:], col["ones_mask"].rearrange("p (a b) -> p a b", a=2)
                                      ).then_inc(xs["cast"], 1)
                nc.vector.tensor_copy(head_sel[:], col["head_row"][0:3 * XH].unsqueeze(2).to_broadcast([3 * XH, XH, P])
                                      ).then_inc(xs["cast"], 1)
                dve.wait_ge(xs["tanh"], 1)
                nc.vector.tensor_tensor(tgx[:], tanhs[:, 0:1], gates[:, 2:3], ALU.mult).then_inc(xs["cast"], 1)
                dve.wait_ge(xs["cast"], 6)
                for h in range(XH):
                    maximum(dve, 0, h)

                def body(b, j, first=False, last=False, ahead=True):
                    def next_maxima(*heads):
                        for h in heads:
                            if not last:
                                maximum(dve, b + 1, h)

                    split_maxima(dve, b)
                    next_maxima(0)
                    keep_maxima(dve, b)
                    if not first:
                        divide(dve, b - 1)
                    next_maxima(1, 2, 3)
                    if ahead:
                        queries(dve, b + 3, (j + 3) % 2)
                    if not first:
                        residual(dve, b - 1)
                    next_maxima(4, 5, 6, 7)

                body(0, 0, first=True)
                dve.wait_ge(xs["inv"], NB // QB)
                with dve.Fori(0, (NB - 4) // RING) as i:
                    for j in range(RING):
                        body(RING * i + 1 + j, (1 + j) % RING)
                def root_args(first, last):
                    dve.wait_ge(xs["mv2"], last)
                    nc.vector.tensor_scalar_add(arg[:, 0, first:last], mv[:, first:last, 1], EPS_LN).then_inc(xs["arg2"], 1)
                    nc.vector.tensor_scalar(arg[:, 1, first:last], mv[:, first:last, 1], 1.0 + EPS_RMS, EPS_RMS * EPS_LN,
                                            ALU.mult, ALU.add).then_inc(xs["arg2"], 1)

                body(NB - 3, (NB - 3) % RING, ahead=False)
                root_args(0, NB - 4)
                body(NB - 2, (NB - 2) % RING, ahead=False)
                body(NB - 1, (NB - 1) % RING, ahead=False, last=True)
                divide(dve, NB - 1)
                residual(dve, NB - 1)
                root_args(NB - 4, NB)

            def scores(pe, b, j, h):
                if h == 0:
                    pe.wait_ge(s_ld[j], 24 * (b - j) + 96)
                if h >= 2 or later(b):
                    pe.wait_ge(xs["max"], XH * b + h - 1)
                for t in range(2):
                    last = nc.tensor.matmul(sc_b[h % 2][:, t * XL:(t + 1) * XL], q_stack[:, j, h, t * P:(t + 1) * P],
                                            k_stack[:, j, h], start=True, stop=True)
                last.then_inc(xs["scores"], 1)

            def transpose_values(pe, b, j):
                if later(b):
                    pe.wait_ge(xs["mt"], b)
                pe.wait_ge(xs["k_split"], 4 * b + 4)
                for t in range(2):
                    for c in range(3):
                        last = nc.tensor.matmul(vt_b[:, t * P:(t + 1) * P], k_parts[:, j, c, t * P:(t + 1) * P], ident16[:],
                                                start=(c == 0), stop=(c == 2))
                last.then_inc(xs["vtp"], 1)

            def transpose_maxima(pe, b):
                pe.wait_ge(xs["max_split"], 4 * b + 4)
                pe.wait_ge(xs["vt"], 2 * b + 2)
                for t in range(2):
                    last = nc.tensor.matmul(mt_b[:, t * P:(t + 1) * P], max_parts[:, t].rearrange("p c h -> p (c h)"),
                                            ident16[:], start=True, stop=True)
                last.then_inc(xs["mtp"], 1)

            def shifted_scores(pe, b, j, unit):
                if unit == 0:
                    pe.wait_ge(xs["mt"], b + 1)
                if unit >= 2 or later(b):
                    pe.wait_ge(xs["exp"], 4 * b + unit - 1)
                for n, h in enumerate(heads_of(unit)):
                    bank = t_b[unit % 2][:, n]
                    for t in range(2):
                        nc.tensor.matmul(bank[:, t * XL:(t + 1) * XL], k_stack[:, j, h, t * P:(t + 1) * P],
                                         q_stack[:, j, h], start=(t == 0), stop=False, skip_group_check=True)
                    for t in range(2):
                        last = nc.tensor.matmul(bank[:, t * XL:(t + 1) * XL], head_sel[:, h], max_t[:],
                                                start=False, stop=(t == 1), skip_group_check=True)
                last.then_inc(xs["tscores"], 1)

            def weigh_values(pe, b, u, par):
                pe.wait_ge(xs["exp"], 4 * b + 2 * par + 2)
                if par == 0 and later(b):
                    pe.wait_ge(xs["ret"], b)
                for t in range(2):
                    for strip in range(4):
                        r = 32 * strip
                        nc.tensor.matmul(pv_b[r:r + 32, 0:XL], v_t[:, u, par, t, r:r + 32],
                                         probs[:, 2 * par + strip // 2, strip % 2, t],
                                         start=(par == 0 and t == 0), stop=(par == 1 and t == 1), skip_group_check=True)
                for t in range(2):
                    for strip in range(4):
                        r = 32 * strip
                        last = nc.tensor.matmul(pv_b[r:r + 32, XL:2 * XL], ones_par[:, par],
                                                probs[:, 2 * par + strip // 2, strip % 2, t],
                                                start=False, stop=(par == 1 and t == 1), skip_group_check=True)
                last.then_inc(xs["pv"], 1)

            @block.tensor
            def _(pe):
                pe.wait_ge(xs["cast"], 6)
                transpose_values(pe, 0, 0)
                for h in range(XH):
                    scores(pe, 0, 0, h)

                def body(b, j, first=False, last=False):
                    def ahead(*heads):
                        for h in heads:
                            if not last:
                                scores(pe, b + 1, (j + 1) % RING, h)

                    ahead(0)
                    if first:
                        pe.wait_ge(xs["setup"], 3)
                    else:
                        weigh_values(pe, b - 1, (j + 1) % 2, 1)
                    ahead(1)
                    transpose_maxima(pe, b)
                    shifted_scores(pe, b, j, 0)
                    shifted_scores(pe, b, j, 1)
                    ahead(2, 3)
                    shifted_scores(pe, b, j, 2)
                    weigh_values(pe, b, j % 2, 0)
                    ahead(4, 5)
                    shifted_scores(pe, b, j, 3)
                    if not last:
                        transpose_values(pe, b + 1, (j + 1) % RING)
                    ahead(6, 7)

                body(0, 0, first=True)
                with pe.Fori(0, (NB - 4) // RING) as i:
                    for j in range(RING):
                        body(RING * i + 1 + j, (1 + j) % RING)
                for b in range(NB - 3, NB):
                    body(b, b % RING, last=(b == NB - 1))
                weigh_values(pe, NB - 1, 1, 1)

            def exponentials(act, b, unit):
                act.wait_ge(xs["tscores"], 4 * b + unit + 1)
                if later(b):
                    act.wait_ge(xs["pv"], 2 * b - 1 + unit // 2)
                nc.scalar.activation(probs[:, unit], t_b[unit % 2].rearrange("p j (t l) -> p j t l", t=2), ACT.Exp,
                                     scale=XD ** -0.5).then_inc(xs["exp"], 1)

            def keep_values(act, b, u):
                act.wait_ge(xs["vtp"], b + 1)
                if later(b, 2):
                    act.wait_ge(xs["pv"], 2 * b - 2)
                for par in range(NPAR):
                    src = vt_b.rearrange("p (t j n) -> p t j n", t=2, j=4)
                    dst = v_t[:, u, par].rearrange("p t (j n) -> p t j n", j=4)
                    nc.scalar.copy(dst[:, :, :, par * XD:par * XD + XD], src[:, :, :, par * XD:par * XD + XD]
                                   ).then_inc(xs["vt"], 1)

            @block.scalar
            def _(act):
                act.dma_start(tab[:], consts).then_inc(s_tab, 16)
                for j in range(RING):
                    act.dma_start(ctx_sb[:, j], ctx_in[j]).then_inc(s_ctx[j], 16)
                for n, g in enumerate((g_xattn, g_ffn, gamma)):
                    act.dma_start(gates[:, n:n + 1], g.partition_broadcast(P)).then_inc(s_in, 16)
                act.dma_start(lnw[:, 0], ln1_w).then_inc(s_in, 16)
                act.dma_start(lnw[:, 1], ln2_w).then_inc(s_in, 16)
                act.dma_start(bias_sb[:], bias_e.partition_broadcast(P)).then_inc(s_in, 16)
                act.wait_ge(s_in, 6 * 16)
                nc.scalar.activation(tanhs[:], gates[:, 0:2], ACT.Tanh).then_inc(xs["tanh"], 1)
                act.wait_ge(xs["setup"], 3)
                keep_values(act, 0, 0)

                def body(b, j):
                    exponentials(act, b, 0)
                    if not isinstance(b, int):
                        act.wait_ge(xs["k_split"], 4 * b)
                        act.dma_start(ctx_sb[:, (j + 3) % RING], ctx_in[b + 3]).then_inc(s_ctx[(j + 3) % RING], 16)
                    exponentials(act, b, 1)
                    if later(b) and not (isinstance(b, int) and b + 2 >= NB):
                        load_stacks(act, b + 2, (j + 2) % RING)
                    exponentials(act, b, 2)
                    if not isinstance(b, int) or b + 1 < NB:
                        keep_values(act, b + 1, (j + 1) % 2)
                    exponentials(act, b, 3)
                    if not isinstance(b, int) or b + 3 < NB:
                        store_parts(act, b + 3, (j + 3) % RING)

                body(0, 0)
                with act.Fori(0, (NB - 4) // RING) as i:
                    for j in range(RING):
                        body(RING * i + 1 + j, (1 + j) % RING)
                for b in range(NB - 3, NB):
                    body(b, b % RING)
        nc.all_engine_barrier()

        gu = sb("gu", [P, E + 1, KT, 2 * I])
        dn = sb("dn", [P, E + 1, H])
        oh_all = sb("oh_all", [P, NB, TOPK, E])
        slots_all = sb("slots_all", [P, NB, TOPK])
        rw_all = sb("rw_all", [P, NB, TOPK])
        counts = sb("counts", [P, E])
        counts16 = sb("counts16", [P, E], BF16)
        tick_v = sb("tick_v", [P, 2])
        tick_p = sb("tick_p", [P, 3])
        wsem = sem("moe_weights")
        wsem2 = sem("moe_weights2")
        s_sh = [sem(f"shared_rows{i}") for i in range(2)]
        s_sc = [sem(f"scattered{i}") for i in range(2)]

        def hold_v():
            nc.vector.tensor_copy(tick_v[:, 0:1], tick_v[:, 1:2])

        def hold_p(u=0):
            return nc.gpsimd.tensor_tensor(tick_p[:, u:u + 1], tick_p[:, 2:3], tick_p[:, 2:3], ALU.add)

        def load_expert_weights(sp, lo, hi, done):
            sp.dma_start(gu[:, lo:hi, :, 0:I], weg[lo:hi].rearrange("e (t p) i -> p (e t) i", p=P)).then_inc(done, 16)
            sp.dma_start(gu[:, lo:hi, :, I:2 * I], weu[lo:hi].rearrange("e (t p) i -> p (e t) i", p=P)).then_inc(done, 16)

        EARLY = E // 2

        with ExitStack() as pf:
            def fsb(name, shape, dt=F32):
                return pf.enter_context(nc.sbuf_tensor(name, shape, dt))

            late = gu[:, EARLY:E].rearrange("p e t n -> p (e t n)")
            q_t = late[:, 0:2 * HQ * S].rearrange("p (u h s) -> p u h s", u=2, h=HQ)
            o_t = late[:, 4096:4096 + HQ * S].rearrange("p (h s) -> p h s", h=HQ)
            k_t = late[:, 6144:6144 + 2 * HKV * S].rearrange("p (u h s) -> p u h s", u=2, h=HKV)
            v_sb = fsb("v_sb", [P, 2, HKV * D])
            wo_sb = fsb("wo_sb", [P, HQ, H])
            zr = fsb("zr", [P, H])
            h_t = fsb("h_t", [P, KT, S])
            r_cos = fsb("r_cos", [P, GQ * D])
            r_sin = fsb("r_sin", [P, GQ * D])
            roped = fsb("roped", [P, 2, GQ * D])
            pr = fsb("pr", [P, 2, GQ, S])
            pn = fsb("pn", [P, GQ, S])
            p_t = fsb("p_t", [P, GQ, S])
            negmax = fsb("fnegmax", [P, 2, GQ])
            sums = fsb("sums", [P, 2, GQ])
            rsums = fsb("rsums", [P, GQ])
            z = fsb("z", [P, H])
            r2 = fsb("r2", [P, H])
            xn = fsb("xn", [P, 2, H])
            xf_t = fsb("xf_t", [P, KT, S])
            rms_arg = fsb("rms_arg", [P, 2])
            rms_inv = fsb("rms_inv", [P, 1])
            rneg = fsb("rneg", [P, 1])
            rsum = fsb("rsum", [P, 1])
            rrec = fsb("rrec", [P, 1])
            rexp = fsb("rexp", [P, E])
            biased = fsb("biased", [P, E])
            top8 = fsb("top8", [P, 8])
            idx8 = fsb("idx8", [P, 8], U32)
            idxf = fsb("idxf", [P, TOPK])
            oh = fsb("oh", [P, TOPK, E])
            mask16 = fsb("mask16", [P, E], BF16)
            both = fsb("both", [P, 2, E])
            prod = fsb("prod", [P, 2, TOPK, E])
            picked = fsb("picked", [P, 2, TOPK])
            islot = fsb("islot", [P, 2, TOPK], I32)
            wsum = fsb("wsum", [P, 1])
            wmax = fsb("wmax", [P, 1])
            wrec = fsb("wrec", [P, 1])

            fs = {n: sem("f_" + n) for n in (
                "wo", "init", "pool_init", "zr", "htp", "ht", "proj", "cs", "rope", "v", "tp", "qk", "s", "max", "exp", "rinv",
                "norm", "ptp", "pt", "otp", "ot", "y", "resid", "rstd", "xn", "rtp", "rt", "logit", "rmax", "rexp",
                "route", "prefix", "slot", "mix", "weights")}
            block = pf.enter_context(nc.Block())
            pj_b, tp_b, pt_b, s_b, o_b, m_b = (banks[:, 0], banks[:, 1]), banks[:, 2], banks[:, 3], \
                (banks[:, 4], banks[:, 5]), banks[:, 6], banks[:, 7]

            @block.sync
            def _(sp):
                sp.dma_start(wo_sb[:], wo.rearrange("(h d) n -> d h n", d=D)).then_inc(fs["wo"], 16)
                sp.dma_start(gu[:, E, :, 0:I], wsg.rearrange("(t p) i -> p t i", p=P)).then_inc(wsem, 16)
                sp.dma_start(gu[:, E, :, I:2 * I], wsu.rearrange("(t p) i -> p t i", p=P)).then_inc(wsem, 16)
                sp.dma_start(dn[:, E], wsd).then_inc(wsem, 16)
                load_expert_weights(sp, 0, EARLY, wsem)
                sp.dma_start(dn[:, 0:E], wed.rearrange("e i h -> i e h")).then_inc(wsem, 16)

            def pe_head_transpose(pe, b):
                pe.wait_ge(fs["zr"], b + 1)
                if later(b):
                    pe.wait_ge(fs["qk"], 5 * b)
                for t in range(KT):
                    last = nc.tensor.transpose(tp_b[:, t * P:(t + 1) * P], zr[:, t * P:(t + 1) * P], ident)
                last.then_inc(fs["htp"], 1)

            def pe_project(pe, b, c):
                if c == 0:
                    pe.wait_ge(fs["ht"], 2 * b + 2)
                if c == 0 and later(b):
                    pe.wait_ge(fs["cs"], 10 * b - 2)
                if c == 1 and later(b):
                    pe.wait_ge(fs["cs"], 10 * b)
                if c == 2:
                    pe.wait_ge(fs["cs"], 10 * b + 2)
                if c == 3:
                    pe.wait_ge(fs["v"], b + 1)
                if c >= 4:
                    pe.wait_ge(fs["cs"], 10 * b + 2 * (c - 2))
                w = (wk_sb, wv_sb)[c] if c < 2 else wq_sb
                at = max(c - 2, 0) * GQ * D
                for t in range(KT):
                    last = nc.tensor.matmul(pj_b[c % 2], h_t[:, t], w[:, t, at:at + GQ * D], start=(t == 0), stop=(t == KT - 1))
                last.then_inc(fs["proj"], 1)

            def pe_chunk_transpose(pe, b, r):
                pe.wait_ge(fs["rope"], 5 * b + r + 1)
                if r == 0:
                    pe.wait_ge(fs["ht"], 2 * b + 2)
                else:
                    pe.wait_ge(fs["qk"], 5 * b + r)
                for j in range(GQ):
                    last = nc.tensor.transpose(tp_b[:, j * P:(j + 1) * P], roped[:, r % 2, j * D:(j + 1) * D], ident)
                last.then_inc(fs["tp"], 1)

            def pe_scores(pe, b, u, g):
                if g == 0:
                    pe.wait_ge(fs["qk"], 5 * b + 5)
                if g >= 2:
                    pe.wait_ge(fs["exp"], 16 * b + 4 * (g - 1))
                elif later(b):
                    pe.wait_ge(fs["exp"], 16 * b - 8 + 4 * (g + 1))
                nc.tensor.matmul(s_b[g % 2].rearrange("p (h s) -> p h s", h=GQ), ident16[:],
                                 causal16[:].unsqueeze(1).to_broadcast([P, GQ, S]), start=True, stop=False)
                for j in range(GQ):
                    last = nc.tensor.matmul(s_b[g % 2][:, j * S:(j + 1) * S], q_t[:, u, g * GQ + j], k_t[:, u, g],
                                            start=False, stop=(j == GQ - 1))
                last.then_inc(fs["s"], 1)

            def pe_probs_transpose(pe, b, g):
                pe.wait_ge(fs["norm"], 4 * b + g + 1)
                if g or later(b):
                    pe.wait_ge(fs["pt"], 4 * b + g)
                for j in range(GQ):
                    last = nc.tensor.transpose(pt_b[:, j * S:(j + 1) * S], pn[:, j], ident)
                last.then_inc(fs["ptp"], 1)

            def pe_weigh(pe, b, u, g):
                pe.wait_ge(fs["pt"], 4 * b + g + 1)
                if g or later(b):
                    pe.wait_ge(fs["ot"], 4 * b + g)
                nc.tensor.matmul(o_b, v_sb[:, u, g * D:(g + 1) * D], p_t[:].rearrange("p h s -> p (h s)"),
                                 start=True, stop=True).then_inc(fs["otp"], 1)

            def pe_out(pe, b, lo, hi):
                if lo == 0:
                    if later(b):
                        pe.wait_ge(fs["slot"], 3 * b - 2)
                    else:
                        pe.wait_ge(fs["wo"], 16)
                pe.wait_ge(fs["ot"], 4 * b + hi // GQ)
                for h in range(lo, hi):
                    last = nc.tensor.matmul(m_b[:, 0:H], o_t[:, h], wo_sb[:, h], start=(h == 0), stop=(h == HQ - 1))
                if hi == HQ:
                    last.then_inc(fs["y"], 1)

            def pe_router_transpose(pe, b, u):
                pe.wait_ge(fs["xn"], b + 1)
                for t in range(KT):
                    last = nc.tensor.transpose(m_b[:, H + t * P:H + (t + 1) * P], xn[:, u, t * P:(t + 1) * P], ident)
                last.then_inc(fs["rtp"], 1)

            def pe_logits(pe, b):
                pe.wait_ge(fs["rt"], 2 * b + 2)
                for t in range(KT):
                    last = nc.tensor.matmul(m_b[:, 0:E], xf_t[:, t], gate_sb[:, t], start=(t == 0), stop=(t == KT - 1))
                last.then_inc(fs["logit"], 1)

            def pe_prefix(pe, b):
                pe.wait_ge(fs["route"], 8 * b + 8)
                pe.wait_ge(fs["rexp"], b + 1)
                nc.tensor.matmul(m_b[:, 0:E], before16[:], mask16[:], start=True, stop=False)
                nc.tensor.matmul(m_b[:, 0:E], ones16[:], counts16[:], start=False, stop=True).then_inc(fs["prefix"], 1)

            def act_copy_scaled(dst, src, w, done):
                for t in range(KT):
                    nc.scalar.activation(dst[:, t], src[:, t * P:(t + 1) * P], ACT.Copy, scale=lnw[:, w, t:t + 1]
                                         ).then_inc(done, 1)

            def act_head_transpose(act, b):
                act.wait_ge(fs["htp"], b + 1)
                if later(b):
                    act.wait_ge(fs["proj"], 6 * b)
                act_copy_scaled(h_t, tp_b, 0, fs["ht"])

            def act_router_transpose(act, b):
                act.wait_ge(fs["rtp"], b + 1)
                if later(b):
                    act.wait_ge(fs["logit"], b)
                act_copy_scaled(xf_t, m_b[:, H:2 * H], 1, fs["rt"])

            def act_values(act, b, u):
                act.wait_ge(fs["proj"], 6 * b + 2)
                if later(b, 2):
                    act.wait_ge(fs["otp"], 4 * b - 4)
                nc.scalar.copy(v_sb[:, u], pj_b[1]).then_inc(fs["v"], 1)

            def act_chunk(act, b, u, r):
                act.wait_ge(fs["tp"], 5 * b + r + 1)
                if later(b, 2):
                    act.wait_ge(fs["s"], 4 * b - 4)
                dst = k_t[:, u] if r == 0 else q_t[:, u, (r - 1) * GQ:r * GQ]
                nc.scalar.copy(dst.rearrange("p h s -> p (h s)"), tp_b).then_inc(fs["qk"], 1)

            def act_exp(act, b, g):
                act.wait_ge(fs["max"], 4 * b + g + 1)
                if g >= 2:
                    act.wait_ge(fs["norm"], 4 * b + g - 1)
                elif later(b):
                    act.wait_ge(fs["norm"], 4 * b + g - 1)
                for j in range(GQ):
                    nc.scalar.activation(pr[:, g % 2, j], s_b[g % 2][:, j * S:(j + 1) * S], ACT.Exp,
                                         bias=negmax[:, g % 2, j:j + 1], accum_out=sums[:, g % 2, j:j + 1]
                                         ).then_inc(fs["exp"], 1)

            def act_probs(act, b, g):
                act.wait_ge(fs["ptp"], 4 * b + g + 1)
                if g or later(b):
                    act.wait_ge(fs["otp"], 4 * b + g)
                nc.scalar.copy(p_t[:].rearrange("p h s -> p (h s)"), pt_b).then_inc(fs["pt"], 1)

            def act_weighed(act, b, g):
                act.wait_ge(fs["otp"], 4 * b + g + 1)
                if later(b):
                    act.wait_ge(fs["y"], b)
                nc.scalar.copy(o_t[:, g * GQ:(g + 1) * GQ].rearrange("p h s -> p (h s)"), o_b).then_inc(fs["ot"], 1)

            def act_route(act, b):
                act.wait_ge(fs["rmax"], b + 1)
                nc.scalar.activation(rexp[:], m_b[:, 0:E], ACT.Exp, bias=rneg[:], accum_out=rsum[:]
                                     ).then_inc(fs["rexp"], 1)

            def dve_norm_rows(dve, b):
                if later(b):
                    dve.wait_ge(fs["htp"], b)
                nc.vector.tensor_scalar(zr[:], x1[:, b, :], mv[:, b, 0:1], inv[:, 1, bass.ds(b, 1)], ALU.subtract, ALU.mult
                                        ).then_inc(fs["zr"], 1)

            def dve_rotate(dve, b, r):
                c = 0 if r == 0 else r + 1
                bank = pj_b[c % 2]
                dve.wait_ge(fs["proj"], 6 * b + c + 1)
                if r or later(b):
                    dve.wait_ge(fs["rope"], 5 * b + r)
                cs, sn = ("k_cos", "k_sin") if r == 0 else ("q_cos", "q_sin")
                nc.vector.tensor_tensor(r_cos[:].rearrange("p (h d) -> p h d", h=GQ), bank.rearrange("p (h d) -> p h d", h=GQ),
                                        col[cs].unsqueeze(1).to_broadcast([P, GQ, D]), ALU.mult).then_inc(fs["cs"], 1)
                pairs = "p (h d two) -> p h d two"
                nc.vector.tensor_tensor(
                    r_sin[:].rearrange(pairs, h=GQ, two=2), bank.rearrange(pairs, h=GQ, two=2)[:, :, :, ::-1],
                    col[sn].rearrange("p (d two) -> p d two", two=2).unsqueeze(1).to_broadcast([P, GQ, D // 2, 2]),
                    ALU.mult).then_inc(fs["cs"], 1)

            def dve_max(dve, b, g):
                dve.wait_ge(fs["s"], 4 * b + g + 1)
                nc.vector.tensor_reduce(negmax[:, g % 2], s_b[g % 2].rearrange("p (h s) -> p h s", h=GQ), AX.X, ALU.max,
                                        negate=True).then_inc(fs["max"], 1)

            def dve_normalize(dve, b, g):
                dve.wait_ge(fs["exp"], 16 * b + 4 * g + 4)
                if g or later(b):
                    dve.wait_ge(fs["norm"], 4 * b + g)
                nc.vector.reciprocal(rsums[:], sums[:, g % 2]).then_inc(fs["rinv"], 1)
                dve.wait_ge(fs["rinv"], 4 * b + g + 1)
                if g or later(b):
                    dve.wait_ge(fs["ptp"], 4 * b + g)
                nc.vector.tensor_tensor(pn[:], pr[:, g % 2], rsums[:].unsqueeze(2).to_broadcast([P, GQ, S]), ALU.mult
                                        ).then_inc(fs["norm"], 1)

            def dve_residual(dve, b):
                R = 7 * b
                nc.vector.tensor_scalar(z[:], x1[:, b, :], mv[:, b, 0:1], inv[:, 0, bass.ds(b, 1)], ALU.subtract, ALU.mult
                                        ).then_inc(fs["resid"], 1)
                dve.wait_ge(fs["y"], b + 1)
                dve.wait_ge(fs["resid"], R + 1)
                nc.vector.tensor_tensor(r2[:], m_b[:, 0:H], z[:], ALU.add).then_inc(fs["resid"], 1)
                dve.wait_ge(fs["resid"], R + 2)
                nc.vector.bn_stats(stats[:], r2[:]).then_inc(fs["resid"], 1)
                dve.wait_ge(fs["resid"], R + 3)
                nc.vector.scalar_tensor_tensor(x1[:, b, :], r2[:], tanhs[:, 1:2], x1[:, b, :], ALU.mult, ALU.add
                                               ).then_inc(fs["resid"], 1)
                nc.vector.bn_aggr(mv1[:], stats[:]).then_inc(fs["resid"], 1)
                dve.wait_ge(fs["resid"], R + 5)
                nc.vector.tensor_scalar(rms_arg[:, 0:1], mv1[:, 0:1], mv1[:, 0:1], EPS_RMS, ALU.mult, ALU.add
                                        ).then_inc(fs["resid"], 1)
                dve.wait_ge(fs["resid"], R + 6)
                nc.vector.tensor_tensor(rms_arg[:, 1:2], rms_arg[:, 0:1], mv1[:, 1:2], ALU.add).then_inc(fs["resid"], 1)

            def dve_rms(dve, b, u):
                dve.wait_ge(fs["rstd"], b + 1)
                if later(b, 2):
                    dve.wait_ge(s_sc[u], 32 * (b - u))
                    dve.wait_ge(s_sh[u], 8 * (b - u))
                nc.vector.tensor_scalar(xn[:, u], r2[:], rms_inv[:], None, ALU.mult).then_inc(fs["xn"], 1)

            def dve_router_max(dve, b):
                dve.wait_ge(fs["logit"], b + 1)
                nc.vector.tensor_reduce(rneg[:], m_b[:, 0:E], AX.X, ALU.max, negate=True).then_inc(fs["rmax"], 1)

            def dve_choose(dve, b):
                R = 8 * b
                done = fs["route"]
                dve.wait_ge(fs["rexp"], b + 1)
                nc.vector.reciprocal(rrec[:], rsum[:]).then_inc(done, 1)
                dve.wait_ge(done, R + 1)
                nc.vector.tensor_scalar(both[:, 1], rexp[:], rrec[:], None, ALU.mult).then_inc(done, 1)
                dve.wait_ge(done, R + 2)
                nc.vector.tensor_tensor(biased[:], both[:, 1], bias_sb[:], ALU.add).then_inc(done, 1)
                dve.wait_ge(done, R + 3)
                hold_v()
                nc.vector.max(top8[:], biased[:]).then_inc(done, 1)
                dve.wait_ge(done, R + 4)
                hold_v()
                nc.vector.max_index(idx8[:], top8[:], biased[:]).then_inc(done, 1)
                dve.wait_ge(done, R + 5)
                nc.vector.tensor_copy(idxf[:], idx8[:, 0:TOPK]).then_inc(done, 1)
                dve.wait_ge(done, R + 6)
                nc.vector.tensor_tensor(oh[:], col["iota_e"].unsqueeze(1).to_broadcast([P, TOPK, E]),
                                        idxf[:].unsqueeze(2).to_broadcast([P, TOPK, E]), ALU.is_equal).then_inc(done, 1)
                dve.wait_ge(done, R + 7)
                with nc.allow_low_precision(reason="a sum of ones and zeros that is one or zero"):
                    nc.vector.tensor_reduce(mask16[:], oh[:].rearrange("p k e -> p e k"), AX.X, ALU.add
                                            ).then_inc(done, 1)

            def dve_slots(dve, b, u):
                R = 8 * b
                dve.wait_ge(fs["prefix"], b + 1)
                nc.vector.tensor_tensor(both[:, 0], m_b[:, 0:E], col["region"], ALU.add).then_inc(fs["slot"], 1)
                dve.wait_ge(fs["slot"], 3 * b + 1)
                dve.wait_ge(fs["route"], R + 8)
                nc.vector.tensor_tensor(prod[:], both[:].unsqueeze(2).to_broadcast([P, 2, TOPK, E]),
                                        oh[:].unsqueeze(1).to_broadcast([P, 2, TOPK, E]), ALU.mult).then_inc(fs["mix"], 1)
                nc.vector.tensor_tensor(counts[:], counts[:], mask16[:], ALU.add).then_inc(fs["mix"], 1)
                dve.wait_ge(fs["mix"], 8 * b + 2)
                nc.vector.tensor_reduce(picked[:], prod[:], AX.X, ALU.add).then_inc(fs["mix"], 1)
                nc.vector.tensor_copy(counts16[:], counts[:]).then_inc(fs["mix"], 1)
                dve.wait_ge(fs["mix"], 8 * b + 4)
                if later(b, 2):
                    dve.wait_ge(s_sc[u], 32 * (b - u))
                nc.vector.tensor_copy(islot[:, u], picked[:, 0]).then_inc(fs["slot"], 1)
                nc.vector.tensor_scalar(slots_all[:, b, :], picked[:, 0], 1.0, None, ALU.mult).then_inc(fs["slot"], 1)
                nc.vector.tensor_scalar(oh_all[:, b], oh[:], 1.0, None, ALU.mult).then_inc(fs["mix"], 1)
                nc.vector.tensor_reduce(wsum[:], picked[:, 1], AX.X, ALU.add).then_inc(fs["mix"], 1)
                dve.wait_ge(fs["mix"], 8 * b + 6)
                nc.vector.tensor_scalar(wmax[:], wsum[:], NORM_MIN, None, ALU.max).then_inc(fs["mix"], 1)
                dve.wait_ge(fs["mix"], 8 * b + 7)
                nc.vector.reciprocal(wrec[:], wmax[:]).then_inc(fs["mix"], 1)
                dve.wait_ge(fs["mix"], 8 * b + 8)
                nc.vector.tensor_scalar(rw_all[:, b, :], picked[:, 1], wrec[:], tanhs[:, 1:2], ALU.mult, ALU.mult
                                        ).then_inc(fs["weights"], 1)

            def pool_rotate(pool, b, r):
                pool.wait_ge(fs["cs"], 10 * b + 2 * r + 2)
                if r >= 2:
                    pool.wait_ge(fs["tp"], 5 * b + r - 1)
                elif later(b):
                    pool.wait_ge(fs["tp"], 5 * b + (0 if r == 0 else r - 1))
                nc.gpsimd.tensor_tensor(roped[:, r % 2], r_cos[:], r_sin[:], ALU.add).then_inc(fs["rope"], 1)

            def pool_rms(pool, b):
                pool.wait_ge(fs["resid"], 7 * b + 7)
                nc.gpsimd.tensor_tensor(rms_inv[:], rms_arg[:, 1:2], col["power"][:, 0:1], ALU.pow).then_inc(fs["rstd"], 1)

            def pool_scatter(pool, b, u):
                pool.wait_ge(fs["slot"], 3 * b + 2)
                pool.wait_ge(fs["xn"], b + 1)
                hold_p()
                for k in range(TOPK):
                    nc.gpsimd.indirect_dma_start(
                        out=x_rows, out_offset=bass.IndirectOffsetOnAxis(ap=islot[:, u, k:k + 1].bitcast(U32), axis=0),
                        in_=xn[:, u], in_offset=None).then_inc(s_sc[u], 16)

            def act_shared_rows(act, b, u):
                act.wait_ge(fs["xn"], b + 1)
                act.dma_start(x_rows[SHARED_ROW:SHARED_ROW + T].rearrange("(b p) h -> b p h", p=P)[b], xn[:, u]
                              ).then_inc(s_sh[u], 16)

            @block.tensor
            def _(pe):
                def body(b, u, prep=True, route=True, head=True):
                    pe_scores(pe, b, u, 0)
                    if route:
                        pe_out(pe, b - 1, HQ - GQ, HQ)
                    if prep:
                        pe_head_transpose(pe, b + 1)
                    pe_scores(pe, b, u, 1)
                    if prep:
                        pe_project(pe, b + 1, 0)
                        pe_project(pe, b + 1, 1)
                    pe_probs_transpose(pe, b, 0)
                    if route:
                        pe_router_transpose(pe, b - 1, 1 - u)
                    if prep:
                        pe_project(pe, b + 1, 2)
                    pe_weigh(pe, b, u, 0)
                    pe_scores(pe, b, u, 2)
                    if prep:
                        pe_chunk_transpose(pe, b + 1, 0)
                    pe_probs_transpose(pe, b, 1)
                    if route:
                        pe_logits(pe, b - 1)
                    if prep:
                        pe_project(pe, b + 1, 3)
                    pe_scores(pe, b, u, 3)
                    pe_weigh(pe, b, u, 1)
                    if prep:
                        pe_chunk_transpose(pe, b + 1, 1)
                    pe_probs_transpose(pe, b, 2)
                    if prep:
                        pe_project(pe, b + 1, 4)
                    pe_weigh(pe, b, u, 2)
                    if prep:
                        pe_chunk_transpose(pe, b + 1, 2)
                        pe_project(pe, b + 1, 5)
                    pe_probs_transpose(pe, b, 3)
                    if route:
                        pe_prefix(pe, b - 1)
                    if prep:
                        pe_chunk_transpose(pe, b + 1, 3)
                    pe_out(pe, b, 0, HQ - GQ)
                    pe_weigh(pe, b, u, 3)
                    if prep:
                        pe_chunk_transpose(pe, b + 1, 4)

                pe.wait_ge(s_w, 4 * 16)
                pe.wait_ge(fs["init"], 3)
                pe_head_transpose(pe, 0)
                pe_project(pe, 0, 0)
                pe_project(pe, 0, 1)
                for c in range(2, 6):
                    pe_project(pe, 0, c)
                    pe_chunk_transpose(pe, 0, c - 2)
                pe_chunk_transpose(pe, 0, 4)
                body(0, 0, route=False)
                body(1, 1)
                body(2, 0)
                with pe.Fori(0, (NB - 6) // 2) as i:
                    body(2 * i + 3, 1)
                    body(2 * i + 4, 0)
                body(NB - 3, 1)
                body(NB - 2, 0, head=False)
                body(NB - 1, 1, prep=False, head=False)
                pe_out(pe, NB - 1, HQ - GQ, HQ)
                pe_router_transpose(pe, NB - 1, 1)
                pe_logits(pe, NB - 1)
                pe_prefix(pe, NB - 1)

            @block.scalar
            def _(act):
                def body(b, u, prep=True, route=True, head=True):
                    if prep:
                        act_head_transpose(act, b + 1)
                    act_exp(act, b, 0)
                    act_exp(act, b, 1)
                    if prep:
                        act_values(act, b + 1, 1 - u)
                    act_probs(act, b, 0)
                    if route:
                        act_router_transpose(act, b - 1)
                        act_shared_rows(act, b - 1, 1 - u)
                    act_weighed(act, b, 0)
                    if prep:
                        act_chunk(act, b + 1, 1 - u, 0)
                    act_probs(act, b, 1)
                    act_exp(act, b, 2)
                    if route:
                        act_route(act, b - 1)
                    act_weighed(act, b, 1)
                    if prep:
                        act_chunk(act, b + 1, 1 - u, 1)
                    act_probs(act, b, 2)
                    act_exp(act, b, 3)
                    act_weighed(act, b, 2)
                    if prep:
                        act_chunk(act, b + 1, 1 - u, 2)
                    act_probs(act, b, 3)
                    if prep:
                        act_chunk(act, b + 1, 1 - u, 3)
                    act_weighed(act, b, 3)
                    if prep:
                        act_chunk(act, b + 1, 1 - u, 4)

                act_head_transpose(act, 0)
                act_values(act, 0, 0)
                for r in range(5):
                    act_chunk(act, 0, 0, r)
                body(0, 0, route=False)
                body(1, 1)
                body(2, 0)
                with act.Fori(0, (NB - 6) // 2) as i:
                    body(2 * i + 3, 1)
                    body(2 * i + 4, 0)
                body(NB - 3, 1)
                body(NB - 2, 0, head=False)
                body(NB - 1, 1, prep=False, head=False)
                act_router_transpose(act, NB - 1)
                act_shared_rows(act, NB - 1, 1)
                act_route(act, NB - 1)

            @block.vector
            def _(dve):
                def body(b, u, prep=True, route=True, head=True):
                    dve_max(dve, b, 0)
                    if route:
                        dve_residual(dve, b - 1)
                    dve_max(dve, b, 1)
                    dve_normalize(dve, b, 0)
                    if route:
                        dve_rms(dve, b - 1, 1 - u)
                    if prep:
                        dve_rotate(dve, b + 1, 0)
                    dve_normalize(dve, b, 1)
                    if prep:
                        dve_rotate(dve, b + 1, 1)
                    dve_max(dve, b, 2)
                    if route:
                        dve_router_max(dve, b - 1)
                    if prep:
                        dve_rotate(dve, b + 1, 2)
                    dve_normalize(dve, b, 2)
                    dve_max(dve, b, 3)
                    if route:
                        dve_choose(dve, b - 1)
                    if prep:
                        dve_rotate(dve, b + 1, 3)
                    if head:
                        dve_norm_rows(dve, b + 2)
                    dve_normalize(dve, b, 3)
                    if route:
                        dve_slots(dve, b - 1, 1 - u)
                    if prep:
                        dve_rotate(dve, b + 1, 4)

                nc.vector.memset(counts[:], 0.0).then_inc(fs["init"], 1)
                nc.vector.memset(tick_v[:], 0.0).then_inc(fs["init"], 1)
                nc.vector.memset(counts16[:], 0.0).then_inc(fs["init"], 1)
                dve.wait_ge(fs["init"], 3)
                dve_norm_rows(dve, 0)
                for r in range(5):
                    dve_rotate(dve, 0, r)
                dve_norm_rows(dve, 1)
                body(0, 0, route=False)
                body(1, 1)
                body(2, 0)
                with dve.Fori(0, (NB - 6) // 2) as i:
                    body(2 * i + 3, 1)
                    body(2 * i + 4, 0)
                body(NB - 3, 1)
                body(NB - 2, 0, head=False)
                body(NB - 1, 1, prep=False, head=False)
                dve_residual(dve, NB - 1)
                dve_rms(dve, NB - 1, 1)
                dve_router_max(dve, NB - 1)
                dve_choose(dve, NB - 1)
                dve_slots(dve, NB - 1, 1)

            @block.gpsimd
            def _(pool):
                def body(b, u, prep=True, route=True, head=True):
                    if route:
                        pool_rms(pool, b - 1)
                    if prep:
                        for r in range(5):
                            pool_rotate(pool, b + 1, r)
                    if route:
                        pool_scatter(pool, b - 1, 1 - u)

                nc.gpsimd.memset(tick_p[:], 0.0).then_inc(fs["pool_init"], 1)
                pool.wait_ge(fs["pool_init"], 1)
                for r in range(5):
                    pool_rotate(pool, 0, r)
                body(0, 0, route=False)
                body(1, 1)
                body(2, 0)
                with pool.Fori(0, (NB - 6) // 2) as i:
                    body(2 * i + 3, 1)
                    body(2 * i + 4, 0)
                body(NB - 3, 1)
                body(NB - 2, 0, head=False)
                body(NB - 1, 1, prep=False, head=False)
                pool_rms(pool, NB - 1)
                pool_scatter(pool, NB - 1, 1)
        nc.all_engine_barrier()

        tiles_i = sb("tiles_i", [P, 2, E], I32)
        tiles_e = sb("tiles_e", [P, E])
        ends = sb("ends", [P, E])
        delta = sb("delta", [P, E])
        below = sb("below", [P, 2, E])
        tile_of = sb("tile_of", [P, 4])
        tile_tab = sb("tile_tab", [1, 2, 4 * WORDS], I32)
        pairs = sb("pairs", [1, 2, WORDS])
        words = sb("words", [1, WORDS], I32)
        pad_row = sb("pad_row", [P, E], I32)
        zeros = sb("zeros", [P, H])
        ypos = sb("ypos", [P, NB, TOPK], I32)
        yposf = sb("yposf", [P, NB * TOPK])
        moved = sb("moved", [P, NB * TOPK, E])

        xt_in = sb("xt_in", [P, 4, H])
        xt_t = sb("xt_t", [P, 2, KT, P])
        gate_act = sb("gate_act", [P, 2, I])
        hid = sb("hid", [P, 2, I])
        hid_t = sb("hid_t", [P, 2, P])
        y_out = sb("y_out", [P, 4, H])

        gath = sb("gath", [P, 2, TOPK, H])
        shared = sb("shared", [P, 2, H])
        idx = sb("idx", [P, 2, TOPK], I32)
        acc = sb("acc", [P, 2, H])

        bs = {n: sem("b_" + n) for n in ("plan", "count", "tab", "tabp", "fill", "zero", "pads", "xtp", "xt", "gu", "silu", "hid", "htp",
                                         "ht", "y", "yo", "ypos", "idx", "comb", "planp", "held")}
        s_xl = [sem(f"s_xl{i}") for i in range(4)]
        s_ys = [sem(f"s_ys{i}") for i in range(4)]
        s_g = [sem(f"s_g{i}") for i in range(2)]
        s_s = [sem(f"s_s{i}") for i in range(2)]
        s_o = [sem(f"s_o{i}") for i in range(2)]
        cnt_b = banks[:, 0]
        x_b, gu_b, h_b, y_b = (banks[:, 0], banks[:, 1]), (banks[:, 2], banks[:, 3]), (banks[:, 4], banks[:, 5]), \
            (banks[:, 6], banks[:, 7])
        LAST_SHARED = SHARED_ROW + T - P

        with nc.Block() as block:
            def in_loop(s):
                return not isinstance(s, int)

            @block.sync
            def _(sp):
                sp.wait_ge(bs["plan"], 8)
                sp.wait_ge(bs["zero"], 1)
                with sp.Fori(0, E // 8) as i:
                    _, rows = nc.values_load_multi_w_load_instructions(
                        pad_row[0:1, bass.ds(8 * i, 8)], engines=[mybir.EngineType.SP], min_val=0, max_val=SHARED_ROW - P)
                    for row in rows:
                        sp.dma_start(x_rows[bass.ds(row, P), :], zeros[:]).then_inc(bs["pads"], 16)
                load_expert_weights(sp, EARLY, E, wsem2)

            @block.gpsimd
            def _(pool):
                nc.gpsimd.memset(zeros[:], 0.0).then_inc(bs["zero"], 1)
                pool.wait_ge(bs["tab"], 5)
                for u in range(2):
                    pool.wait_ge(s_sh[u], 8 * NB)

                def load_tiles(s):
                    _, rows = nc.values_load_multi_w_load_instructions(
                        tile_tab[0:1, 1, bass.ds(s + BEFORE, 4)], engines=[mybir.EngineType.Pool], min_val=0, max_val=LAST_SHARED)
                    for j, row in enumerate(rows):
                        if in_loop(s) or s >= 4:
                            pool.wait_ge(bs["xtp"], s + j - 3)
                        pool.dma_start(xt_in[:, j], x_rows[bass.ds(row, P), :]).then_inc(s_xl[j], 16)

                load_tiles(0)
                with pool.Fori(0, NB // 4 - 1) as i:
                    load_tiles(4 * i + 4)
                for u in range(2):
                    pool.wait_ge(s_sc[u], 32 * NB)
                pool.wait_ge(bs["pads"], 16 * E)
                with pool.Fori(0, ROUTED_TILES // 4) as i:
                    load_tiles(4 * i + NB)

                for i in range(4):
                    pool.wait_ge(s_ys[i], 16 * (TILES // 4))

                def gather(b, u):
                    pool.wait_ge(bs["idx"], b + 1)
                    if in_loop(b) or b >= 2:
                        pool.wait_ge(bs["comb"], 5 * b - 5)
                        pool.wait_ge(bs["held"], b - 1)
                    hold_p(u).then_inc(bs["held"], 1)
                    for k in range(TOPK):
                        nc.gpsimd.indirect_dma_start(
                            out=gath[:, u, k], out_offset=None, in_=y_rows,
                            in_offset=bass.IndirectOffsetOnAxis(ap=idx[:, u, k:k + 1].bitcast(U32), axis=0)
                        ).then_inc(s_g[u], 16)

                gather(0, 0)
                gather(1, 1)
                with pool.Fori(0, (NB - 2) // 2) as i:
                    gather(2 * i + 2, 0)
                    gather(2 * i + 3, 1)

            @block.tensor
            def _(pe):
                nc.tensor.matmul(cnt_b[:, 0:E], ones16[:], counts16[:], start=True, stop=True).then_inc(bs["count"], 1)
                pe.wait_ge(bs["planp"], 4)
                for n in range(2):
                    last = nc.tensor.matmul(banks[0:1, 1, n * P:(n + 1) * P], tile_of[:, 2 + n:3 + n], ident,
                                            start=True, stop=True)
                last.then_inc(bs["tabp"], 1)
                pe.wait_ge(bs["tab"], 5)
                pe.wait_ge(wsem, 6 * 16)

                def experts_at(s):
                    _, two = nc.values_load_multi_w_load_instructions(
                        words[0:1, bass.ds(s // 4, 2)], engines=[mybir.EngineType.PE], min_val=0,
                        max_val=(1 << 4 * EBITS) - 1)
                    return [nc.s_assert_within((two[n // 4] >> EBITS * (n % 4)) & ((1 << EBITS) - 1), 0, E,
                                               skip_runtime_bounds_check_because="the table's experts are clamped")
                            for n in range(BEFORE + SKEW)]

                def up(s, j, e):
                    if in_loop(s) or s < TILES:
                        pe.wait_ge(s_xl[j], 4 * (s - j) + 16)
                        if in_loop(s) or s >= 2:
                            pe.wait_ge(bs["xt"], s - 1)
                        for t in range(KT):
                            last = nc.tensor.transpose(x_b[j % 2][:, t * P:(t + 1) * P], xt_in[:, j, t * P:(t + 1) * P], ident)
                        last.then_inc(bs["xtp"], 1)
                    if in_loop(s) or 1 <= s < TILES + 1:
                        pe.wait_ge(bs["xt"], s)
                        if in_loop(s) or s >= 3:
                            pe.wait_ge(bs["hid"], s - 2)
                        for t in range(KT):
                            last = nc.tensor.matmul(gu_b[(j - 1) % 2][:, 0:2 * I], xt_t[:, (j - 1) % 2, t],
                                                    gu[:, bass.ds(e, 1), t, :].rearrange("p a n -> p (a n)"),
                                                    start=(t == 0), stop=(t == KT - 1))
                        last.then_inc(bs["gu"], 1)

                def down(s, j, e):
                    if in_loop(s) or 2 <= s < TILES + 2:
                        pe.wait_ge(bs["hid"], s - 1)
                        if in_loop(s) or s >= 4:
                            pe.wait_ge(bs["ht"], s - 3)
                        nc.tensor.transpose(h_b[j % 2][:, 0:P], hid[:, j % 2], ident).then_inc(bs["htp"], 1)
                    if in_loop(s) or 3 <= s:
                        pe.wait_ge(bs["ht"], s - 2)
                        if in_loop(s) or s >= 5:
                            pe.wait_ge(bs["yo"], s - 4)
                        nc.tensor.matmul(y_b[(j - 1) % 2][:, 0:H], hid_t[:, (j - 1) % 2],
                                         dn[:, bass.ds(e, 1), :].rearrange("p a n -> p (a n)"), start=True, stop=True
                                         ).then_inc(bs["y"], 1)

                def steps(s, n=4):
                    of = experts_at(s)
                    if in_loop(s) or s:
                        down(s - 1, 3, of[0])
                    for j in range(n):
                        up(s + j, j, of[3 + j])
                        if j < 3:
                            down(s + j, j, of[1 + j])

                steps(0)
                steps(4)
                with pe.Fori(0, (NB + EARLY) // 4 - 2) as i:
                    steps(4 * i + 8)
                pe.wait_ge(wsem2, 32)
                with pe.Fori(0, (TILES - NB - EARLY) // 4) as i:
                    steps(4 * i + NB + EARLY)
                steps(TILES, SKEW)

            @block.scalar
            def _(act):
                def step(s, j):
                    if in_loop(s) or 1 <= s < TILES + 1:
                        act.wait_ge(bs["gu"], s)
                        if in_loop(s) or s >= 3:
                            act.wait_ge(bs["hid"], s - 2)
                        nc.scalar.activation(gate_act[:, (j - 1) % 2], gu_b[(j - 1) % 2][:, 0:I], ACT.Silu
                                             ).then_inc(bs["silu"], 1)
                    if in_loop(s) or 2 <= s < TILES + 2:
                        act.wait_ge(bs["htp"], s - 1)
                        if in_loop(s) or s >= 4:
                            act.wait_ge(bs["y"], s - 3)
                        nc.scalar.copy(hid_t[:, j % 2], h_b[j % 2][:, 0:P]).then_inc(bs["ht"], 1)
                    if in_loop(s) or 3 <= s:
                        i = (j - 3) % 4
                        act.wait_ge(bs["y"], s - 2)
                        if in_loop(s) or s >= 7:
                            act.wait_ge(s_ys[i], 4 * (s - 3 - i))
                        nc.scalar.copy(y_out[:, i], y_b[(j - 1) % 2][:, 0:H]).then_inc(bs["yo"], 1)
                        at = y_tiles[s - 3]
                        act.wait_ge(bs["yo"], s - 2)
                        act.dma_start(at, y_out[:, i]).then_inc(s_ys[i], 16)

                y_tiles = y_rows.rearrange("(t p) h -> t p h", p=P)
                for s in range(8):
                    step(s, s % 4)
                with act.Fori(0, TILES // 4 - 2) as i:
                    for j in range(4):
                        step(4 * i + 8 + j, j)
                for s in range(TILES, TILES + SKEW):
                    step(s, s % 4)

                for i in range(4):
                    act.wait_ge(s_ys[i], 16 * (TILES // 4))

                def move(b, u, ahead=True):
                    act.wait_ge(bs["comb"], 5 * b + 5)
                    act.dma_start(out[b], acc[:, u]).then_inc(s_o[u], 16)
                    if ahead:
                        act.dma_start(shared[:, u], y_tiles[b + 2]).then_inc(s_s[u], 16)

                act.dma_start(shared[:, 0], y_tiles[0]).then_inc(s_s[0], 16)
                act.dma_start(shared[:, 1], y_tiles[1]).then_inc(s_s[1], 16)
                with act.Fori(0, (NB - 2) // 2) as i:
                    move(2 * i, 0)
                    move(2 * i + 1, 1)
                move(NB - 2, 0, ahead=False)
                move(NB - 1, 1, ahead=False)
                for u in range(2):
                    act.wait_ge(s_o[u], 16 * (NB // 2))

            @block.vector
            def _(dve):
                plan, planp = bs["plan"], bs["planp"]
                dve.wait_ge(bs["count"], 1)
                nc.vector.tensor_scalar(tiles_i[:, 0], cnt_b[:, 0:E], float(P - 1), None, ALU.add).then_inc(plan, 1)
                nc.vector.tensor_tensor(pad_row[:], cnt_b[:, 0:E], col["region"], ALU.add).then_inc(plan, 1)
                dve.wait_ge(plan, 1)
                nc.vector.tensor_single_scalar(tiles_i[:, 1], tiles_i[:, 0], 7, ALU.arith_shift_right).then_inc(plan, 1)
                dve.wait_ge(plan, 3)
                nc.vector.tensor_copy(tiles_e[:], tiles_i[:, 1]).then_inc(plan, 1)
                dve.wait_ge(plan, 4)
                nc.vector.tensor_tensor_scan(ends[:], tiles_e[:], tiles_e[:], 0.0, ALU.add, ALU.bypass).then_inc(plan, 1)
                dve.wait_ge(plan, 5)
                nc.vector.tensor_scalar(below[:, 0], ends[:], col["tile_no"], None, ALU.is_le).then_inc(plan, 1)
                nc.vector.tensor_tensor(delta[:], ends[:], tiles_e[:], ALU.subtract).then_inc(plan, 1)
                dve.wait_ge(plan, 7)
                nc.vector.tensor_tensor(below[:, 1], below[:, 0], tiles_e[:], ALU.mult).then_inc(plan, 1)
                dve.wait_ge(plan, 8)
                nc.vector.tensor_reduce(tile_of[:, 0:2], below[:], AX.X, ALU.add).then_inc(planp, 1)
                dve.wait_ge(planp, 1)
                nc.vector.tensor_tensor(tile_of[:, 1:2], col["tile_no"], tile_of[:, 1:2], ALU.subtract).then_inc(planp, 1)
                nc.vector.tensor_scalar(tile_of[:, 2:3], tile_of[:, 0:1], float(E - 1), None, ALU.min).then_inc(planp, 1)
                dve.wait_ge(planp, 3)
                nc.vector.tensor_scalar(tile_of[:, 0:1], tile_of[:, 0:1], float(REGION // P), None, ALU.mult
                                        ).then_inc(bs["ypos"], 1)
                dve.wait_ge(bs["ypos"], 1)
                nc.vector.tensor_scalar(tile_of[:, 3:4], tile_of[:, 0:1], tile_of[:, 1:2], float(LAST_SHARED // P), ALU.add,
                                        ALU.min).then_inc(planp, 1)
                nc.vector.tensor_scalar(tile_tab[:, 0], tab[0:1, 0:4 * WORDS], 0.0, float(E), ALU.mult, ALU.add
                                        ).then_inc(bs["fill"], 1)
                nc.vector.tensor_scalar(tile_tab[:, 1, BEFORE:BEFORE + NB], col["tile_no_row"][0:1], float(P), float(SHARED_ROW),
                                        ALU.mult, ALU.add).then_inc(bs["fill"], 1)
                dve.wait_ge(bs["tabp"], 1)
                dve.wait_ge(bs["fill"], 2)
                from_bank = banks[0:1, 1, 0:2 * P].rearrange("p (a t) -> p a t", a=2)[:, :, 0:ROUTED_TILES]
                nc.vector.tensor_copy(tile_tab[:, 0, BEFORE + NB:BEFORE + TILES], from_bank[:, 0]).then_inc(bs["tab"], 1)
                nc.vector.tensor_scalar(tile_tab[:, 1, BEFORE + NB:BEFORE + TILES], from_bank[:, 1], float(P), None, ALU.mult
                                        ).then_inc(bs["tab"], 1)
                dve.wait_ge(bs["tab"], 2)
                by_four = tile_tab[:, 0].rearrange("p (w n) -> p w n", n=4)
                for n in range(2):
                    nc.vector.scalar_tensor_tensor(pairs[:, n], by_four[:, :, 2 * n + 1], float(1 << EBITS),
                                                   by_four[:, :, 2 * n], ALU.mult, ALU.add).then_inc(bs["tab"], 1)
                dve.wait_ge(bs["tab"], 4)
                nc.vector.scalar_tensor_tensor(words[:], pairs[:, 1], float(1 << 2 * EBITS), pairs[:, 0], ALU.mult, ALU.add
                                               ).then_inc(bs["tab"], 1)
                nc.vector.tensor_scalar(delta[:], delta[:], float(P), float(NB * P), ALU.mult, ALU.add
                                        ).then_inc(bs["ypos"], 1)
                dve.wait_ge(bs["ypos"], 2)
                nc.vector.tensor_tensor(delta[:], delta[:], col["region"], ALU.subtract).then_inc(bs["ypos"], 1)

                def positions():
                    dve.wait_ge(bs["ypos"], 3)
                    nc.vector.tensor_tensor(moved[:], oh_all[:].rearrange("p b k e -> p (b k) e"),
                                            delta[:].unsqueeze(1).to_broadcast([P, NB * TOPK, E]), ALU.mult
                                            ).then_inc(bs["ypos"], 1)
                    dve.wait_ge(bs["ypos"], 4)
                    nc.vector.tensor_reduce(yposf[:], moved[:], AX.X, ALU.add).then_inc(bs["ypos"], 1)
                    dve.wait_ge(bs["ypos"], 5)
                    nc.vector.tensor_tensor(ypos[:].rearrange("p b k -> p (b k)"), yposf[:],
                                            slots_all[:].rearrange("p b k -> p (b k)"), ALU.add).then_inc(bs["ypos"], 1)

                def step(s, j):
                    if in_loop(s) or s < TILES:
                        dve.wait_ge(bs["xtp"], s + 1)
                        if in_loop(s) or s >= 2:
                            dve.wait_ge(bs["gu"], s - 1)
                        nc.vector.tensor_tensor(xt_t[:, j % 2], x_b[j % 2][:, 0:H].rearrange("p (t n) -> p t n", t=KT),
                                                lnw[:, 1].unsqueeze(2).to_broadcast([P, KT, P]), ALU.mult
                                                ).then_inc(bs["xt"], 1)
                    if in_loop(s) or 1 <= s < TILES + 1:
                        dve.wait_ge(bs["silu"], s)
                        if in_loop(s) or s >= 3:
                            dve.wait_ge(bs["htp"], s - 2)
                        nc.vector.tensor_tensor(hid[:, (j - 1) % 2], gu_b[(j - 1) % 2][:, I:2 * I], gate_act[:, (j - 1) % 2],
                                                ALU.mult).then_inc(bs["hid"], 1)

                for s in range(8):
                    step(s, s % 4)
                positions()
                with dve.Fori(0, TILES // 4 - 2) as i:
                    for j in range(4):
                        step(4 * i + 8 + j, j)
                step(TILES, 0)

                def indices(b, u):
                    if in_loop(b) or b >= 2:
                        dve.wait_ge(s_g[u], 32 * (b - u))
                    nc.vector.tensor_scalar(idx[:, u], ypos[:, b, :], 1.0, None, ALU.mult).then_inc(bs["idx"], 1)

                def combine(b, u, ahead=True):
                    dve.wait_ge(s_s[u], 8 * (b - u) + 16)
                    if in_loop(b) or b >= 2:
                        dve.wait_ge(s_o[u], 8 * (b - u))
                    nc.vector.scalar_tensor_tensor(acc[:, u], shared[:, u], tanhs[:, 1:2], x1[:, b, :], ALU.mult, ALU.add
                                                   ).then_inc(bs["comb"], 1)
                    dve.wait_ge(s_g[u], 32 * (b - u) + 64)
                    for k in range(TOPK):
                        dve.wait_ge(bs["comb"], 5 * b + k + 1)
                        nc.vector.scalar_tensor_tensor(acc[:, u], gath[:, u, k], rw_all[:, b, k:k + 1], acc[:, u], ALU.mult,
                                                       ALU.add).then_inc(bs["comb"], 1)
                    if ahead:
                        indices(b + 2, u)

                dve.wait_ge(bs["ypos"], 6)
                indices(0, 0)
                indices(1, 1)
                combine(0, 0)
                combine(1, 1)
                with dve.Fori(0, (NB - 4) // 2) as i:
                    combine(2 * i + 2, 0)
                    combine(2 * i + 3, 1)
                combine(NB - 2, 0, ahead=False)
                combine(NB - 1, 1, ahead=False)


def kernel(x, ctx_2048, g_xattn, g_ffn, L0_xattn_gamma, L0_ffn_ln1_w, L0_ffn_ln2_w, L0_ffn_wq, L0_ffn_wk, L0_ffn_wv,
           L0_ffn_wo, L0_ffn_gate_w, L0_ffn_bias_e, L0_ffn_weg, L0_ffn_weu, L0_ffn_wed, L0_ffn_wsg, L0_ffn_wsu,
           L0_ffn_wsd):
    import concourse.bacc as bacc
    from concourse.bass_utils import run_bass_kernel_spmd

    def by_channel(w):
        return np.asarray(w).reshape(KT, P).T

    arrays = {
        "x": x, "ctx": ctx_2048, "g_xattn": g_xattn, "g_ffn": g_ffn, "gamma": np.asarray(L0_xattn_gamma).reshape(1),
        "ln1_w": by_channel(L0_ffn_ln1_w), "ln2_w": by_channel(L0_ffn_ln2_w), "wq": L0_ffn_wq, "wk": L0_ffn_wk,
        "wv": L0_ffn_wv, "wo": L0_ffn_wo,
        "gate_wt": np.asarray(L0_ffn_gate_w).T.reshape(KT, P, E).transpose(1, 0, 2), "bias_e": L0_ffn_bias_e,
        "weg": L0_ffn_weg, "weu": L0_ffn_weu, "wed": L0_ffn_wed, "wsg": L0_ffn_wsg, "wsu": L0_ffn_wsu,
        "wsd": L0_ffn_wsd, "consts": constant_table(),
    }
    nc = bacc.Bacc("TRN2", target_bir_lowering=False, num_devices=1)
    feeds, args = {}, []
    for name, a in arrays.items():
        a = np.ascontiguousarray(a)
        feeds[f"in_{name}"] = a
        args.append(nc.dram_tensor(f"in_{name}", a.shape, mybir.dt.from_np(a.dtype), kind="ExternalInput").ap())
    out = nc.dram_tensor("out_x", (NB, S, H), F32, kind="ExternalOutput").ap()
    build(nc, *args, out)
    r = run_bass_kernel_spmd(nc, [feeds], core_ids=[0])
    return r.results[0]["out_x"]
```
